# Optimizing a Trainium2 kernel written in Bass

```python
import numpy as np
import jax
import jax.numpy as jnp

def _softmax(x, axis=-1):
    return jax.nn.softmax(x, axis=axis)

def _gelu(x):
    return jax.nn.gelu(x, approximate=True)

def _silu(x):
    return jax.nn.silu(x)

def _sigmoid(x):
    return jax.nn.sigmoid(x)

def _layernorm(x, axis=-1, eps=1e-05):
    m = jnp.mean(x, axis=axis, keepdims=True)
    v = jnp.var(x, axis=axis, keepdims=True)
    return (x - m) / jnp.sqrt(v + eps)

def _scatter_add(tgt, idx, src, axis=0):
    return tgt.at[idx].add(src)

def _segment_sum(src, seg, n):
    return jax.ops.segment_sum(src, seg, n)
kernel_name = 'mk_conv_preact_d2_conv_nchw512_r2_c85ee6'

def setup_inputs(seed: int=0):
    np.random.seed(seed)
    _w = jnp.asarray

    def _rec_inputs():
        import jax
        import jax.numpy as jnp
        _gk = jax.random.key(seed)
        x = -0.000125 + 0.9999 * jax.random.normal(jax.random.fold_in(_gk, 1), (16, 256, 32, 32), jnp.float32)
        return x
    x = _rec_inputs()

    def _L0_conv_setup():
        import jax, jax.numpy as jnp
        import numpy as np
        THRESHOLD = 0.625
        key = jax.random.key(seed)
        k1, k2 = jax.random.split(key)
        x = jax.random.normal(k1, (16, 256, 32, 32), dtype=jnp.float32)
        negative_dict = 0.02 * jax.random.truncated_normal(k2, -2.0, 2.0, (256, 256), dtype=jnp.float32)
        return {'x': x, 'negative_dict': negative_dict}
    _L0_conv_all = _L0_conv_setup()
    _L0_conv_in = {k: v for k, v in _L0_conv_all.items() if k in ('negative_dict',)}
    del _L0_conv_all

    def _L1_conv_setup():
        import jax, jax.numpy as jnp
        from jax import lax
        import numpy as np
        INPUT_DIM = 256
        OUTPUT_DIM = 256
        D_STATE = 16
        D_CONV = 4
        EXPAND = 2
        D_MODEL = INPUT_DIM // 4
        D_INNER = EXPAND * D_MODEL
        DT_RANK = (D_MODEL + 15) // 16
        EPS = 1e-05

        def layer_norm(x, g, b):
            mu = jnp.mean(x, axis=-1, keepdims=True)
            var = jnp.mean((x - mu) ** 2, axis=-1, keepdims=True)
            return (x - mu) * lax.rsqrt(var + EPS) * g + b

        def mamba(x, in_proj_w, conv_w, conv_b, x_proj_w, dt_proj_w, dt_proj_b, A_log, D_param, out_proj_w):
            Beff, L, _ = x.shape
            xz = jnp.einsum('bld,ed->ble', x, in_proj_w)
            xi, z = jnp.split(xz, 2, axis=-1)
            xc = lax.conv_general_dilated(xi.transpose(0, 2, 1), conv_w[:, None, :], (1,), [(D_CONV - 1, 0)], feature_group_count=D_INNER)
            xc = jax.nn.silu(xc + conv_b[None, :, None]).transpose(0, 2, 1)
            dbc = jnp.einsum('bld,ed->ble', xc, x_proj_w)
            dt = dbc[..., :DT_RANK]
            Bs = dbc[..., DT_RANK:DT_RANK + D_STATE]
            Cs = dbc[..., DT_RANK + D_STATE:]
            dt = jax.nn.softplus(jnp.einsum('blr,er->ble', dt, dt_proj_w) + dt_proj_b)
            A = -jnp.exp(A_log)

            def step(h, inp):
                dt_t, B_t, C_t, x_t = inp
                dA = jnp.exp(dt_t[:, :, None] * A)
                h = dA * h + (dt_t * x_t)[:, :, None] * B_t[:, None, :]
                y = jnp.einsum('bds,bs->bd', h, C_t)
                return (h, y)
            h0 = jnp.zeros((Beff, D_INNER, D_STATE), x.dtype)
            _, ys = lax.scan(step, h0, (dt.transpose(1, 0, 2), Bs.transpose(1, 0, 2), Cs.transpose(1, 0, 2), xc.transpose(1, 0, 2)))
            y = ys.transpose(1, 0, 2) + xc * D_param
            y = y * jax.nn.silu(z)
            return jnp.einsum('bld,od->blo', y, out_proj_w)
        key = jax.random.key(seed)
        ks = jax.random.split(key, 10)
        inp = {'x': jax.random.normal(ks[0], (4, INPUT_DIM, 32, 32), jnp.float32), 'norm_g': jnp.ones((INPUT_DIM,), jnp.float32), 'norm_b': jnp.zeros((INPUT_DIM,), jnp.float32), 'in_proj_w': jax.random.normal(ks[1], (2 * D_INNER, D_MODEL), jnp.float32) * 0.02, 'conv_w': jax.random.normal(ks[2], (D_INNER, D_CONV), jnp.float32) * 0.2, 'conv_b': jnp.zeros((D_INNER,), jnp.float32), 'x_proj_w': jax.random.normal(ks[3], (DT_RANK + 2 * D_STATE, D_INNER), jnp.float32) * 0.02, 'dt_proj_w': jax.random.normal(ks[4], (D_INNER, DT_RANK), jnp.float32) * 0.1, 'dt_proj_b': jnp.full((D_INNER,), -2.0, jnp.float32), 'A_log': jnp.log(jnp.broadcast_to(jnp.arange(1, D_STATE + 1, dtype=jnp.float32), (D_INNER, D_STATE))), 'D_param': jnp.ones((D_INNER,), jnp.float32), 'out_proj_w': jax.random.normal(ks[5], (D_MODEL, D_INNER), jnp.float32) * 0.02, 'proj_w': jax.random.normal(ks[6], (OUTPUT_DIM, INPUT_DIM), jnp.float32) * 0.02, 'proj_b': jnp.zeros((OUTPUT_DIM,), jnp.float32), 'skip_scale': jnp.ones((1,), jnp.float32)}
        return inp
    _L1_conv_all = _L1_conv_setup()
    _L1_conv_in = {k: v for k, v in _L1_conv_all.items() if k in ('norm_g', 'norm_b', 'in_proj_w', 'conv_w', 'conv_b', 'x_proj_w', 'dt_proj_w', 'dt_proj_b', 'A_log', 'D_param', 'out_proj_w', 'proj_w', 'proj_b', 'skip_scale')}
    del _L1_conv_all
    return {'x': x, 'L0_conv_negative_dict': _L0_conv_in['negative_dict'], 'L1_conv_norm_g': _L1_conv_in['norm_g'], 'L1_conv_norm_b': _L1_conv_in['norm_b'], 'L1_conv_in_proj_w': _L1_conv_in['in_proj_w'], 'L1_conv_conv_w': _L1_conv_in['conv_w'], 'L1_conv_conv_b': _L1_conv_in['conv_b'], 'L1_conv_x_proj_w': _L1_conv_in['x_proj_w'], 'L1_conv_dt_proj_w': _L1_conv_in['dt_proj_w'], 'L1_conv_dt_proj_b': _L1_conv_in['dt_proj_b'], 'L1_conv_A_log': _L1_conv_in['A_log'], 'L1_conv_D_param': _L1_conv_in['D_param'], 'L1_conv_out_proj_w': _L1_conv_in['out_proj_w'], 'L1_conv_proj_w': _L1_conv_in['proj_w'], 'L1_conv_proj_b': _L1_conv_in['proj_b'], 'L1_conv_skip_scale': _L1_conv_in['skip_scale']}

def reference(x, L0_conv_negative_dict, L1_conv_norm_g, L1_conv_norm_b, L1_conv_in_proj_w, L1_conv_conv_w, L1_conv_conv_b, L1_conv_x_proj_w, L1_conv_dt_proj_w, L1_conv_dt_proj_b, L1_conv_A_log, L1_conv_D_param, L1_conv_out_proj_w, L1_conv_proj_w, L1_conv_proj_b, L1_conv_skip_scale):
    import jax
    import jax.numpy as jnp

    def _L0_conv_ref(x, negative_dict):
        import jax, jax.numpy as jnp
        import numpy as np
        THRESHOLD = 0.625
        f_norm = x / jnp.linalg.norm(x, axis=1, keepdims=True)
        d_norm = negative_dict / jnp.linalg.norm(negative_dict, axis=1, keepdims=True)
        sim = jnp.einsum('bchw,nc->bnhw', f_norm, d_norm)
        dist = (1.0 - sim) * 0.5
        apm = jnp.min(dist, axis=1, keepdims=True)
        index = jnp.argmin(dist, axis=1)
        replace_map = (apm < THRESHOLD).astype(x.dtype)
        restructured = negative_dict[index]
        restructured = jnp.transpose(restructured, (0, 3, 1, 2))
        out = x * (1.0 - replace_map) + restructured * replace_map
        return out

    def _L1_conv_ref(x, norm_g, norm_b, in_proj_w, conv_w, conv_b, x_proj_w, dt_proj_w, dt_proj_b, A_log, D_param, out_proj_w, proj_w, proj_b, skip_scale):
        import jax, jax.numpy as jnp
        from jax import lax
        import numpy as np
        INPUT_DIM = 256
        OUTPUT_DIM = 256
        D_STATE = 16
        D_CONV = 4
        EXPAND = 2
        D_MODEL = INPUT_DIM // 4
        D_INNER = EXPAND * D_MODEL
        DT_RANK = (D_MODEL + 15) // 16
        EPS = 1e-05

        def layer_norm(x, g, b):
            mu = jnp.mean(x, axis=-1, keepdims=True)
            var = jnp.mean((x - mu) ** 2, axis=-1, keepdims=True)
            return (x - mu) * lax.rsqrt(var + EPS) * g + b

        def mamba(x, in_proj_w, conv_w, conv_b, x_proj_w, dt_proj_w, dt_proj_b, A_log, D_param, out_proj_w):
            Beff, L, _ = x.shape
            xz = jnp.einsum('bld,ed->ble', x, in_proj_w)
            xi, z = jnp.split(xz, 2, axis=-1)
            xc = lax.conv_general_dilated(xi.transpose(0, 2, 1), conv_w[:, None, :], (1,), [(D_CONV - 1, 0)], feature_group_count=D_INNER)
            xc = jax.nn.silu(xc + conv_b[None, :, None]).transpose(0, 2, 1)
            dbc = jnp.einsum('bld,ed->ble', xc, x_proj_w)
            dt = dbc[..., :DT_RANK]
            Bs = dbc[..., DT_RANK:DT_RANK + D_STATE]
            Cs = dbc[..., DT_RANK + D_STATE:]
            dt = jax.nn.softplus(jnp.einsum('blr,er->ble', dt, dt_proj_w) + dt_proj_b)
            A = -jnp.exp(A_log)

            def step(h, inp):
                dt_t, B_t, C_t, x_t = inp
                dA = jnp.exp(dt_t[:, :, None] * A)
                h = dA * h + (dt_t * x_t)[:, :, None] * B_t[:, None, :]
                y = jnp.einsum('bds,bs->bd', h, C_t)
                return (h, y)
            h0 = jnp.zeros((Beff, D_INNER, D_STATE), x.dtype)
            _, ys = lax.scan(step, h0, (dt.transpose(1, 0, 2), Bs.transpose(1, 0, 2), Cs.transpose(1, 0, 2), xc.transpose(1, 0, 2)))
            y = ys.transpose(1, 0, 2) + xc * D_param
            y = y * jax.nn.silu(z)
            return jnp.einsum('bld,od->blo', y, out_proj_w)
        B, C, H, W = x.shape
        L = H * W
        xf = x.reshape(B, C, L).transpose(0, 2, 1)
        xn = layer_norm(xf, norm_g, norm_b)
        chunks = xn.reshape(B, L, 4, D_MODEL).transpose(2, 0, 1, 3).reshape(4 * B, L, D_MODEL)
        ym = mamba(chunks, in_proj_w, conv_w, conv_b, x_proj_w, dt_proj_w, dt_proj_b, A_log, D_param, out_proj_w)
        ym = ym + skip_scale * chunks
        y = ym.reshape(4, B, L, D_MODEL).transpose(1, 2, 0, 3).reshape(B, L, C)
        y = layer_norm(y, norm_g, norm_b)
        y = jnp.einsum('blc,oc->blo', y, proj_w) + proj_b
        return y.transpose(0, 2, 1).reshape(B, OUTPUT_DIM, H, W)

    def _gn(v, G=32, eps=1e-05):
        B_, C_, H_, W_ = v.shape
        g = v.reshape(B_, G, C_ // G, H_, W_)
        m = jnp.mean(g, axis=(2, 3, 4), keepdims=True)
        s = jnp.var(g, axis=(2, 3, 4), keepdims=True)
        return ((g - m) / jnp.sqrt(s + eps)).reshape(v.shape)

    def _ln_c(v, eps=1e-06):
        m = jnp.mean(v, axis=1, keepdims=True)
        s = jnp.var(v, axis=1, keepdims=True)
        return (v - m) / jnp.sqrt(s + eps)

    def _ln_t(v, eps=1e-05):
        m = jnp.mean(v, axis=-1, keepdims=True)
        s = jnp.var(v, axis=-1, keepdims=True)
        return (v - m) / jnp.sqrt(s + eps)

    def _to_tokens(v):
        B_, C_, H_, W_ = v.shape
        return v.reshape(B_, C_, H_ * W_).transpose(0, 2, 1)

    def _from_tokens(t, like):
        B_, C_, H_, W_ = like.shape
        return t.transpose(0, 2, 1).reshape(B_, C_, H_, W_)
    x = x + _L0_conv_ref(_gn(x), L0_conv_negative_dict)
    x = x + _L1_conv_ref(_gn(x), L1_conv_norm_g, L1_conv_norm_b, L1_conv_in_proj_w, L1_conv_conv_w, L1_conv_conv_b, L1_conv_x_proj_w, L1_conv_dt_proj_w, L1_conv_dt_proj_b, L1_conv_A_log, L1_conv_D_param, L1_conv_out_proj_w, L1_conv_proj_w, L1_conv_proj_b, L1_conv_skip_scale)
    return x

_drawn_inputs = setup_inputs


def setup_inputs(seed=0):
    import zlib

    import numpy as np

    out = dict(_drawn_inputs(seed))
    spreads = {'L1_conv_norm_g': (1.0, 0.2),
     'L1_conv_norm_b': (0.0, 0.1),
     'L1_conv_conv_b': (0.0, 0.8),
     'L1_conv_dt_proj_b': (-2.0, 0.6),
     'L1_conv_D_param': (1.0, 0.6),
     'L1_conv_proj_b': (0.0, 0.1)}
    factors = {'L0_conv_negative_dict': 3.298,
     'L1_conv_in_proj_w': 8.0,
     'L1_conv_conv_w': 8.0,
     'L1_conv_x_proj_w': 8.0,
     'L1_conv_dt_proj_w': 8.0,
     'L1_conv_A_log': 8.0,
     'L1_conv_out_proj_w': 8.0}
    for name, (base, spread) in spreads.items():
        noise = np.random.default_rng([zlib.crc32(name.encode()), seed]).standard_normal(out[name].shape)
        drawn = base * np.exp(spread * noise) if base else spread * noise
        out[name] = jnp.asarray(drawn.astype(out[name].dtype))
    for name, factor in factors.items():
        out[name] = (out[name] * factor).astype(out[name].dtype)
    return out
```

```python
from contextlib import ExitStack

import concourse.bass as bass
from concourse import mybir

ALU = mybir.AluOpType
ACT = mybir.ActivationFunctionType
F32 = mybir.dt.float32
BF16 = mybir.dt.bfloat16
U32 = mybir.dt.uint32

P = 128
NB = 16
CH = 256
NJ = CH // P
L = 1024
HALF = 512
NC = 4
DM = CH // NC
NS = 16
SEQ_STEPS = 2 * NS
NT = L // P
WORDS = 256
PAD = 3
LN_EPS = 1e-5
GN_EPS = 1e-5
E_MAX = float(2.0 ** 60)

C_CONVB, C_DTB, C_D, C_ALOG, C_G, C_B, C_PB, C_SKIP, N_COLS = 0, 1, 2, 3, 19, 21, 23, 25, 26

BUF_OF_STATE = [0, 1, 2] * 5 + [1]
BANK_OF_STEP = [0, 1, 2] * 10 + [0, 1]


def last_use(order, i):
    d = 1
    while order[(i - d) % len(order)] != order[i]:
        d += 1
    return i - d


def at_least(eng, sem, value):
    if isinstance(value, int) and value <= 0:
        return
    eng.wait_ge(sem, value)


PE_SEQ = {8: ["prep_xc0"], 9: ["prep_xc1"], 11: ["prep_z0"], 12: ["prep_z1"], 14: ["post_out0"],
          15: ["post_out1"], 18: ["prep_bc0"], 19: ["prep_bc1"], 22: ["prep_dt0"], 23: ["prep_dt1"]}
ACT_SEQ = {9: ["prep_xc0"], 10: ["prep_xc1"], 12: ["prep_z0"], 13: ["prep_z1", "prep_sig_x"],
           16: ["prep_sig_z"], 19: ["prep_hi0"], 20: ["prep_hi1"], 22: ["prep_mid"], 23: ["prep_dt0"],
           24: ["prep_dt1"], 25: ["prep_dt_exp"], 26: ["prep_dt_ln"]}
DVE_SEQ = {6: ["post_y"], 11: ["prep_clamp_x"], 14: ["prep_clamp_z"], 15: ["post_skip0"], 16: ["post_skip1"],
           20: ["prep_rest0"], 21: ["prep_rest1"], 27: ["prep_dt"]}
POOL_SEQ = {10: ["prep_silu_x"], 14: ["prep_silu_z"], 20: ["prep_lo"], 27: ["prep_u"]}
PE_BATCH = {(0, 3): ["a_group0"], (0, 17): ["a_norm"], (0, 26): ["a_sim00"], (0, 27): ["a_sim01"],
            (0, 28): ["a_sim10"], (0, 29): ["a_sim11"], (0, 30): ["a_sim20"], (0, 31): ["a_sim21"],
            (1, 0): ["a_sim30"], (1, 1): ["a_sim31"], (1, 3): ["c_mean0"], (1, 4): ["c_square0"],
            (1, 6): ["c_mean1"], (1, 7): ["c_square1"], (1, 26): ["a_turn0"], (1, 27): ["a_turn1"],
            (1, 29): ["a_keep0"], (1, 30): ["a_word00"], (1, 31): ["a_word01"], (2, 0): ["a_keep1"],
            (2, 1): ["a_word10"], (2, 3): ["a_word11"], (2, 17): ["a_group1"], (2, 26): ["a_mean0"],
            (2, 27): ["a_square0"], (2, 29): ["a_mean1"], (2, 30): ["a_square1"],
            (3, 0): ["c_proj00"], (3, 1): ["c_proj01"], (3, 3): ["c_proj10"], (3, 4): ["c_proj11"]}
ACT_BATCH = {(0, 5): ["a_rstd0"], (0, 7): ["a_affine00"], (0, 8): ["a_affine01"], (0, 18): ["a_rn"],
             (0, 21): ["c_sq0"], (0, 23): ["c_sq1"],
             (1, 4): ["c_ln0"], (1, 7): ["c_ln1"], (1, 27): ["a_oht0"], (1, 28): ["a_oht1"],
             (2, 19): ["a_rstd1"], (2, 21): ["a_affine10"], (2, 23): ["a_affine11"], (2, 27): ["a_ln0"],
             (2, 30): ["a_ln1"], (3, 2): ["a_xn0"], (3, 3): ["a_xn1"]}
DVE_BATCH = {(0, 0): ["a_stat00"], (0, 1): ["a_stat01"], (0, 4): ["a_mom0"], (0, 6): ["a_newton0"],
             (0, 28): ["a_pick0"], (0, 30): ["a_pick1"], (1, 0): ["a_pick2"], (1, 2): ["a_pick3"],
             (1, 5): ["c_ln0"], (1, 8): ["c_ln1"],
             (1, 30): ["a_keep0"], (1, 31): ["a_mix00"], (2, 0): ["a_mix01"], (2, 1): ["a_keep1"],
             (2, 2): ["a_mix10"], (2, 4): ["a_mix11"], (2, 13): ["a_stat10"], (2, 14): ["a_stat11"],
             (2, 18): ["a_mom1"], (2, 20): ["a_newton1"], (2, 28): ["a_ln0"], (2, 31): ["a_ln1"],
             (3, 1): ["c_out00"], (3, 2): ["c_out01"], (3, 4): ["c_out10"], (3, 5): ["c_out11"]}
POOL_BATCH = {(0, 12): ["a_xg"], (1, 5): ["c_scale0"], (1, 8): ["c_scale1"], (2, 4): ["a_x2"],
              (2, 29): ["a_scale0"], (2, 31): ["a_scale1"]}
SP_BATCH = {(0, 0): ["x_in", "x2_back"], (0, 5): ["xs3"], (2, 4): ["x2_store"], (3, 4): ["xs0", "xs1", "xs2"],
            (3, 9): ["out"]}
SUM_AT = [8 + r - (r >= 11) - (r >= 22) for r in range(SEQ_STEPS)]

FIRST, LOOP, LAST = "first", "loop", "last"


def plan(seq_plan, batch_plan, kind, c, j):
    names = []
    for name in seq_plan.get(j, []):
        if name.startswith("post") and kind == FIRST and c == 0:
            continue
        if name.startswith("prep") and kind == LAST and c == NC - 1:
            continue
        names.append(name)
    for name in batch_plan.get((c, j), []):
        if kind == FIRST and (name in ("x2_back", "out") or name.startswith("c_")):
            continue
        if kind == LAST and (name.startswith("a_") or name in ("x_in", "x2_store", "xs0", "xs1", "xs2")):
            continue
        names.append(name)
    return names


SINGLE = {"a_group0": 0, "a_norm": 0, "a_sim00": 0, "a_sim10": 1, "a_sim20": 0, "a_sim30": 1,
          "a_turn0": 0, "a_turn1": 1, "a_keep0": 0, "a_word00": 1, "a_word01": 0, "a_keep1": 1,
          "a_word10": 0, "a_word11": 1, "a_group1": 0}


def bank_use(name, c):
    if name.startswith(("prep", "post")):
        return [(int(name[-1]), (name, c))]
    if name in SINGLE:
        return [(SINGLE[name], (name, 0))]
    if name.startswith("a_sim"):
        return []
    if name.startswith("c_proj"):
        return [(int(name[-1]), (name, 0))]
    return [(0 if "mean" in name else 1, (name, 0))]


SETUP_USES = [(0, "dtw"), (1, "pb")] + [(i % 2, ("word", i)) for i in range(4)]
STATS = ["mean0", "square0", "mean1", "square1"]
A_ALL = (["a_group0", "a_norm"] + [f"a_sim{i}{k}" for i in range(4) for k in range(2)]
         + ["a_turn0", "a_turn1", "a_keep0", "a_word00", "a_word01", "a_keep1", "a_word10", "a_word11", "a_group1"]
         + ["a_" + w for w in STATS])
PREP_ALL = [f"prep_{w}{h}" for w in ("xc", "z", "bc", "dt") for h in range(2)]
C_STATS = ["c_" + w for w in STATS]
C_PROJ = [f"c_proj{h}{m}" for h in range(2) for m in range(NJ)]


class Banks:

    def __init__(self):
        self.at, self.count = {}, {}
        self.note("pro", SETUP_USES + [u for n in A_ALL for u in bank_use(n, 0)]
                  + [u for n in PREP_ALL for u in bank_use(n, NC - 1)])
        for kind in (FIRST, LOOP, LAST):
            self.note(kind, [u for c in range(NC) for j in range(SEQ_STEPS)
                             for n in plan(PE_SEQ, PE_BATCH, kind, c, j) for u in bank_use(n, c)])
        self.note("tail", [u for n in ["post_out0", "post_out1"] + C_STATS + C_PROJ for u in bank_use(n, 0)])

    def note(self, kind, uses):
        n = [0, 0]
        for bank, key in uses:
            self.at[kind, key] = (bank, n[bank])
            n[bank] += 1
        self.count[kind] = n

    def __call__(self, kind, b, key):
        bank, place = self.at[kind, key]
        before = 0
        if kind != "pro":
            before = self.count["pro"][bank]
        if kind in (LOOP, LAST, "tail"):
            before += self.count[FIRST][bank]
        if kind == LOOP:
            before = self.count[LOOP][bank] * (b - 1) + before
        if kind in (LAST, "tail"):
            before += self.count[LOOP][bank] * (NB - 2)
        if kind == "tail":
            before += self.count[LAST][bank]
        return bank, before + place + 1


def build(nc, x, words, cols, w_in, w_z, w_taps, w_x, w_dt, w_xdt, w_out, w_proj,
          iota, ident_f, ident_b, group_mean, select, out):
    x_v = x.rearrange("b (j p) h w -> b p j (h w)", p=P)
    out_v = out.rearrange("b (j p) h w -> b p j (h w)", p=P)
    x2_v = nc.dram_tensor("x2_scratch", (NB, P, NJ, L), F32).ap()
    banks = Banks()

    with ExitStack() as ctx:
        def sb(name, shape, dt=F32):
            return ctx.enter_context(nc.sbuf_tensor(name, shape, dt))

        def ps(name, shape):
            return ctx.enter_context(nc.psum_tensor(name, shape, F32))

        def sem(name):
            return ctx.enter_context(nc.semaphore(name))

        bx = ps("bx", [P, 3, HALF])
        cb = ps("cb", [P, HALF])
        yp = ps("yp", [P, 2, HALF])
        mb = ps("mb", [P, 2, HALF])

        dt = sb("dt", [P, 2, L])
        u = sb("u", [P, 2, L])
        xc = sb("xc", [P, 2, L])
        zz = sb("zz", [P, 2, L])
        bc = sb("bc", [96, 2, L], BF16)
        decay = sb("decay", [P, 3, L])
        c_sb = sb("c_sb", [P, 2, L])
        state = sb("state", [P, 3, L])
        hc = sb("hc", [P, 3, L])
        xs = sb("xs", [P, NC, L + PAD + 1])
        e_x = sb("e_x", [P, L])
        e_z = sb("e_z", [P, L])
        rest = sb("rest", [96, L])
        mid = sb("mid", [96, L], BF16)
        yy = sb("yy", [P, L])
        ym = sb("ym", [P, NJ, L])
        cd = sb("cd", [P, NJ, L])
        res = sb("res", [P, NJ, L])
        xt = sb("xt", [P, NJ, L])
        gt = sb("gt", [P, NJ, L])
        xn = sb("xn", [P, NJ, L])
        hot_t = sb("hot_t", [P, 2, L], BF16)
        sim = sb("sim", [P, 2, WORDS])
        best = sb("best", [P, 2, 8])
        where = sb("where", [P, 2, 8], U32)
        wheref = sb("wheref", [P, 2])
        close = sb("close", [P, 2])
        hot = sb("hot", [P, NT, WORDS], BF16)
        rn_l = sb("rn_l", [P, NT])
        rn = sb("rn", [P, NT])
        stats = sb("stats", [P, NJ, 2, 6])
        mv = sb("mv", [P, NJ, 2])
        gs = sb("gs", [P, 2, NJ])
        gm = sb("gm", [P, 2, NJ])
        gsm = sb("gsm", [P, 8, NJ])
        sq_a = sb("sq_a", [P, HALF])
        rs_a = sb("rs_a", [P, HALF])
        sq_c = sb("sq_c", [P, HALF])
        rs_c = sb("rs_c", [P, HALF])
        col = sb("col", [P, N_COLS])
        a_neg = sb("a_neg", [P, NS])
        ncb = sb("ncb", [P, 1])
        pb2 = sb("pb2", [P, NJ])
        wtap = sb("wtap", [P, 2, P])
        wz = sb("wz", [DM, P])
        wx = sb("wx", [P, 96])
        wdt4 = sb("wdt4", [4, 2, P])
        wdt = sb("wdt", [P, P])
        wo = sb("wo", [P, DM])
        wp = sb("wp", [P, NJ, CH])
        idf = sb("idf", [P, P])
        idb = sb("idb", [P, P], BF16)
        oneb = sb("oneb", [P, P], BF16)
        mean_w = sb("mean_w", [P, P])
        onef = sb("onef", [P, 1])
        grp = sb("grp", [P, P])
        sel = sb("sel", [96, 2 * NS, P], BF16)
        iot = sb("iot", [P, WORDS])
        word_hml = sb("word_hml", [P, 3, 2, CH], BF16)
        wordn_t = sb("wordn_t", [P, NJ, WORDS])
        wn = sb("wn", [P, 8, 2])
        word_f = cd[:, 0, 0:512].rearrange("p (k c) -> p k c", k=2)
        word_n = cd[:, 1, 0:512].rearrange("p (k c) -> p k c", k=2)
        word_r = res[:, 0, 0:512].rearrange("p (k c) -> p k c", k=2)
        word_q = res[:, 1, 0:512].rearrange("p (k c) -> p k c", k=2)
        w_in_f = ym[:, 0, 0:P]
        taps_f = ym[:, 0, P:3 * P].rearrange("p (k d) -> p k d", k=2)

        s_w = sem("weights_in")
        s_x = sem("x_in")
        s_xs = [sem(f"xs_in{c}") for c in range(NC)]
        s_x2st = sem("x2_stored")
        s_x2ld = sem("x2_back")
        s_out = sem("out_stored")
        m_full = [sem(f"shared_full{i}") for i in range(2)]
        m_free = [sem(f"shared_free{i}") for i in range(2)]
        b_full = sem("b_broadcast")
        bx_done = sem("bx_multiplied")
        scanned = sem("scanned")
        decayed = sem("decay_ready")
        c_full = sem("c_broadcast")
        c_copied = sem("c_copied")
        hc_done = sem("hc_ready")
        summed = sem("y_summed")
        y_taken = sem("y_taken")
        y_gated = sem("y_gated")
        ym_done = sem("ym_ready")
        x_pre = sem("x_pre")
        x_clamped = sem("x_clamped")
        x_ln = sem("x_ln")
        x_sig = sem("x_sig")
        x_silu = sem("x_silu")
        z_pre = sem("z_pre")
        z_clamped = sem("z_clamped")
        z_ln = sem("z_ln")
        z_sig = sem("z_sig")
        z_silu = sem("z_silu")
        bc_hi = sem("bc_hi")
        bc_rest = sem("bc_rest")
        bc_mid = sem("bc_mid")
        bc_lo = sem("bc_lo")
        dt_abs = sem("dt_abs")
        dt_exp = sem("dt_exp")
        v_dt = sem("dve_softplus")
        dt_ln = sem("dt_ln")
        dt_done = sem("dt_ready")
        u_done = sem("u_ready")
        v_stat = [sem(f"dve_stat{g}") for g in range(2)]
        v_mom = [sem(f"dve_moments{g}") for g in range(2)]
        v_newton = [sem(f"dve_newton{g}") for g in range(2)]
        a_rln = [sem(f"rstd_ln{g}") for g in range(2)]
        a_rstd = [sem(f"rstd_guess{g}") for g in range(2)]
        a_aff = [sem(f"normalised{g}") for g in range(2)]
        a_sqd = [sem(f"squared{g}") for g in range(2)]
        xg_done = sem("x_plus_g")
        rn_ln = sem("pixel_norm_ln")
        rn_done = sem("pixel_norm")
        v_pick = sem("dve_pick")
        hot_done = sem("one_hot_ready")
        hot_copied = sem("one_hot_turned")
        g_kept = sem("g_kept")
        g_mixed = sem("g_mixed")
        x2_done = sem("x2_ready")
        al_sq, cl_sq = sem("a_mean_squared"), sem("c_mean_squared")
        al_var, cl_var = sem("a_variance"), sem("c_variance")
        al_ln, cl_ln = sem("a_variance_ln"), sem("c_variance_ln")
        al_rs, cl_rs = sem("a_rstd"), sem("c_rstd")
        al_d, cl_d = sem("a_centred"), sem("c_centred")
        al_n, cl_n = sem("a_scaled"), sem("c_scaled")
        xn_done = sem("xn_ready")
        c_sqd = sem("ym_squared")
        res_done = sem("result_ready")
        su_mem = sem("setup_memset")
        su_dve = sem("setup_dve")
        su_act = sem("setup_act")
        su_pe_ready = sem("setup_for_pe")
        su_words = sem("setup_words")
        su_words_done = sem("setup_words_done")
        su_done = sem("setup_done")

        passed = sem("passed")

        def hold_here(eng):
            eng.sem_inc(passed, 1)

        block = ctx.enter_context(nc.Block())

        @block.sync
        def _(sp):
            def await_(sem_, value):
                if not isinstance(value, int) or value > 0:
                    sp.wait_ge(sem_, value)
                    hold_here(sp)

            loads = [(col[:], cols), (word_f, words.rearrange("(k p) c -> p k c", p=P)), (w_in_f, w_in),
                     (taps_f, w_taps), (wz[:], w_z), (wx[:], w_x), (wdt4[:, 0, :], w_dt), (wdt4[:, 1, :], w_xdt),
                     (wo[:], w_out), (wp[:], w_proj.rearrange("(j p) o -> p j o", p=P)), (idf[:], ident_f),
                     (idb[:], ident_b), (grp[:], group_mean), (sel[:], select), (iot[:], iota)]
            sp.dma_start(xt[:], x_v[0]).then_inc(s_x, 16)
            for dst, src in loads:
                sp.dma_start(dst, src).then_inc(s_w, 16)

            def load_chunk(c, t):
                await_(xn_done, NJ * (t + 1))
                await_(ym_done, 2 * (4 * t + c - 3))
                src = xn[DM * (c % 2):DM * (c % 2) + DM, c // 2, :]
                sp.dma_start(xs[0:DM, c, PAD:PAD + L], src).then_inc(s_xs[c], 16)
                sp.dma_start(xs[DM:P, c, PAD + 1:PAD + 1 + L], src).then_inc(s_xs[c], 16)

            def store_x2(t):
                await_(x2_done, t + 1)
                sp.dma_start(x2_v[t], xt[:]).then_inc(s_x2st, 16)

            def do(name, b):
                t = b + 1
                if name == "x2_back":
                    await_(s_x2st, 16 * b)
                    sp.dma_start(res[:], x2_v[b - 1]).then_inc(s_x2ld, 16)
                elif name == "out":
                    await_(res_done, 4 * b)
                    sp.dma_start(out_v[b - 1], res[:]).then_inc(s_out, 16)
                    await_(s_out, 16 * b)
                elif name == "x_in":
                    await_(a_sqd[1], NJ * t)
                    await_(s_x2st, 16 * t)
                    sp.dma_start(xt[:], x_v[t]).then_inc(s_x, 16)
                elif name == "x2_store":
                    store_x2(b + 1)
                elif name == "xs3":
                    load_chunk(3, b)
                else:
                    load_chunk(int(name[-1]), b + 1)

            def turn(kind, b):
                for c in range(NC):
                    for j in range(SEQ_STEPS):
                        for name in plan({}, SP_BATCH, kind, c, j):
                            do(name, b)

            store_x2(0)
            await_(su_mem, 1)
            for c in range(3):
                load_chunk(c, 0)
            turn(FIRST, 0)
            with sp.Fori(1, NB - 1) as b:
                turn(LOOP, b)
            turn(LAST, NB - 1)
            do("x2_back", NB)
            do("out", NB)

        @block.gpsimd
        def _(pool):
            def do(name, b, c, s=-1):
                m = 4 * b + c + 1
                par = (c + 1) % 2
                if name == "prep_silu_x":
                    pool.wait_ge(x_sig, m + 1)
                    pool.tensor_tensor(xc[:, par, :], xc[:, par, :], e_x[:], ALU.mult).then_inc(x_silu, 1)
                elif name == "prep_silu_z":
                    pool.wait_ge(z_sig, m + 1)
                    pool.tensor_tensor(zz[:, par, :], zz[:, par, :], e_z[:], ALU.mult).then_inc(z_silu, 1)
                elif name == "prep_lo":
                    pool.wait_ge(bc_mid, m + 1)
                    pool.wait_ge(z_silu, m + 1)
                    at_least(pool, hc_done, 16 * m - NS + s + 1)
                    pool.tensor_tensor(bc[64:96, par, :], rest[64:96, :], mid[64:96, :],
                                       ALU.subtract).then_inc(bc_lo, 1)
                    pool.wait_ge(bc_lo, m + 1)
                elif name == "prep_u":
                    pool.wait_ge(dt_done, m + 1)
                    at_least(pool, bx_done, 32 * (m - 1))
                    pool.tensor_tensor(u[:, par, :], dt[:, par, :], xc[:, par, :], ALU.mult).then_inc(u_done, 1)
                elif name == "a_xg":
                    pool.wait_ge(a_sqd[0], NJ * (b + 2))
                    for j in range(NJ):
                        last = pool.tensor_tensor(xt[:, j, :], xt[:, j, :], gt[:, j, :], ALU.add)
                    last.then_inc(xg_done, 1)
                elif name == "a_x2":
                    pool.wait_ge(xg_done, b + 2)
                    pool.wait_ge(g_mixed, 4 * (b + 2))
                    for j in range(NJ):
                        last = pool.tensor_tensor(xt[:, j, :], xt[:, j, :], gt[:, j, :], ALU.add)
                    last.then_inc(x2_done, 1)
                else:
                    h = int(name[-1])
                    tile, rs, s_rs, s_d, done, t = ((gt, rs_a, al_rs, al_d, al_n, b + 1) if name[0] == "a"
                                                    else (cd, rs_c, cl_rs, cl_d, cl_n, b - 1))
                    pool.wait_ge(s_rs, 2 * t + h + 1)
                    pool.wait_ge(s_d, 2 * t + h + 1)
                    for j in range(NJ):
                        v = tile[:, j, h * HALF:(h + 1) * HALF]
                        last = pool.tensor_tensor(v, v, rs[:], ALU.mult)
                    last.then_inc(done, 1)

            def gate(b, c, s):
                n16 = 64 * b + 16 * c
                k = BUF_OF_STATE[s]
                pool.wait_ge(scanned, 2 * n16 + 2 * s + 2)
                pool.wait_ge(c_copied, 2 * n16 + 2 * s + 2)
                at_least(pool, summed, n16 + last_use(BUF_OF_STATE, s) + 1)
                pool.tensor_tensor(hc[:, k, :], state[:, k, :], c_sb[:, s % 2, :], ALU.mult).then_inc(hc_done, 1)

            def turn(kind, b):
                for c in range(NC):
                    for s in range(NS):
                        gate(b, c, s)
                        for h in range(2):
                            for name in plan(POOL_SEQ, POOL_BATCH, kind, c, 2 * s + h):
                                do(name, b, c, s)

            pool.memset(xs[:, :, 0:PAD + 1], 0.0).then_inc(su_mem, 1)
            for name in ("a_xg", "a_x2", "a_scale0", "a_scale1"):
                do(name, -1, 0)
            for name in ("prep_silu_x", "prep_silu_z", "prep_lo", "prep_u"):
                do(name, -1, NC - 1)
            turn(FIRST, 0)
            with pool.Fori(1, NB - 1) as b:
                turn(LOOP, b)
            turn(LAST, NB - 1)
            do("c_scale0", NB, 0)
            do("c_scale1", NB, 0)

        @block.scalar
        def _(act):
            def rsqrt(dst, tmp, src, eps, ln_done, ln_count, done):
                act.activation(tmp, src, ACT.Ln, bias=eps).then_inc(ln_done, 1)
                act.wait_ge(ln_done, ln_count)
                return act.activation(dst, tmp, ACT.Exp, scale=-0.5).then_inc(done, 1)

            def sigmoid(e, clamped, ln_done, done, m):
                act.wait_ge(clamped, m + 1)
                act.activation(e, e, ACT.Ln, bias=1.0).then_inc(ln_done, 1)
                act.wait_ge(ln_done, m + 1)
                act.activation(e, e, ACT.Exp, scale=-1.0).then_inc(done, 1)

            def do(name, kind, b, c):
                m = 4 * b + c + 1
                par = (c + 1) % 2
                t = b + 1
                h = int(name[-1]) if name[-1] in "01" else 0
                cut = slice(h * HALF, (h + 1) * HALF)
                if name.startswith("prep_xc"):
                    at_least(act, u_done, m)
                    at_least(act, dt_done, m)
                    at_least(act, y_taken, m - 1)
                    bank, use = banks(kind, b, (name, c))
                    act.wait_ge(m_full[bank], use)
                    act.activation(e_x[:, cut], mb[:, bank, :], ACT.Exp, bias=ncb[:, 0:1], scale=-1.0).then_inc(x_pre, 1)
                    act.activation(xc[:, par, cut], mb[:, bank, :], ACT.Identity,
                                   bias=col[:, C_CONVB:C_CONVB + 1]).then_inc(m_free[bank], 1)
                elif name.startswith("prep_z"):
                    at_least(act, dt_done, m)
                    at_least(act, y_gated, m - 1)
                    bank, use = banks(kind, b, (name, c))
                    act.wait_ge(m_full[bank], use)
                    act.activation(e_z[:, cut], mb[:, bank, :], ACT.Exp, scale=-1.0).then_inc(z_pre, 1)
                    act.activation(zz[:, par, cut], mb[:, bank, :], ACT.Copy).then_inc(m_free[bank], 1)
                elif name == "prep_sig_x":
                    sigmoid(e_x[:], x_clamped, x_ln, x_sig, m)
                elif name == "prep_sig_z":
                    sigmoid(e_z[:], z_clamped, z_ln, z_sig, m)
                elif name.startswith("prep_hi"):
                    at_least(act, b_full, 32 * (m - 1))
                    at_least(act, c_full, 32 * (m - 1))
                    bank, use = banks(kind, b, (f"prep_bc{h}", c))
                    act.wait_ge(m_full[bank], use)
                    act.activation(bc[:, par, cut], mb[0:96, bank, :], ACT.Copy).then_inc(bc_hi, 1)
                elif name == "prep_mid":
                    act.wait_ge(bc_rest, 2 * (m + 1))
                    at_least(act, bc_lo, m)
                    act.activation(bc[32:64, par, :], rest[32:64, :], ACT.Copy)
                    act.activation(mid[64:96, :], rest[64:96, :], ACT.Copy).then_inc(bc_mid, 1)
                elif name in ("prep_dt0", "prep_dt1"):
                    act.wait_ge(x_silu, m + 1)
                    at_least(act, decayed, 16 * (m - 1))
                    at_least(act, u_done, m - 1)
                    bank, use = banks(kind, b, (name, c))
                    act.wait_ge(m_full[bank], use)
                    act.activation(e_x[:, cut], mb[:, bank, :], ACT.Abs, bias=col[:, C_DTB:C_DTB + 1]).then_inc(dt_abs, 1)
                    act.activation(dt[:, par, cut], mb[:, bank, :], ACT.Identity,
                                   bias=col[:, C_DTB:C_DTB + 1]).then_inc(m_free[bank], 1)
                elif name == "prep_dt_exp":
                    act.wait_ge(dt_abs, 2 * (m + 1))
                    act.activation(e_x[:], e_x[:], ACT.Exp, scale=-1.0).then_inc(dt_exp, 1)
                elif name == "prep_dt_ln":
                    act.wait_ge(dt_exp, m + 1)
                    act.wait_ge(z_silu, m + 1)
                    at_least(act, ym_done, 2 * (m - 1))
                    act.activation(e_z[:], e_x[:], ACT.Identity, bias=1.0)
                    act.activation(yy[:], e_x[:], ACT.Ln, bias=1.0).then_inc(dt_ln, 1)
                elif name.startswith("a_rstd"):
                    g = int(name[-1])
                    act.wait_ge(v_mom[g], 3 * (t + 1))
                    rsqrt(gsm[:, 2, :], gsm[:, 1, :], gsm[:, 0, :], GN_EPS, a_rln[g], t + 1, a_rstd[g])
                elif name.startswith("a_affine"):
                    g, j = int(name[-2]), int(name[-1])
                    act.wait_ge(v_newton[g], 5 * (t + 1))
                    if g == 0:
                        act.wait_ge(s_x, 16 * (t + 1))
                        at_least(act, xn_done, NJ * t)
                        at_least(act, s_x2ld, 16 * b)
                    else:
                        act.wait_ge(x2_done, t + 1)
                        at_least(act, s_xs[3], 32 * t)
                    act.activation((xn if g else cd)[:, j, :], xt[:, j, :], ACT.Square, scale=gsm[:, 4, j:j + 1],
                                   bias=gsm[:, 5, j:j + 1])
                    act.activation(gt[:, j, :], xt[:, j, :], ACT.Identity, scale=gsm[:, 4, j:j + 1],
                                   bias=gsm[:, 5, j:j + 1]).then_inc(a_sqd[g], 1)
                elif name == "a_rn":
                    bank, use = banks(kind, b, ("a_norm", 0))
                    act.wait_ge(m_full[bank], use)
                    at_least(act, hot_done, 4 * t)
                    rsqrt(rn[:], rn_l[:], mb[:, bank, 0:NT], 0.0, rn_ln, t + 1, rn_done)
                    act.sem_inc(m_free[bank], 1)
                elif name.startswith("a_oht"):
                    q = int(name[-1])
                    bank, use = banks(kind, b, (f"a_turn{q}", 0))
                    act.wait_ge(m_full[bank], use)
                    src = mb[:, bank, :].bitcast(BF16).rearrange("p (k t) -> p k t", k=2)
                    act.activation(hot_t[:, :, q * HALF:(q + 1) * HALF], src, ACT.Copy).then_inc(hot_copied, 1)
                    act.wait_ge(hot_copied, 2 * t + q + 1)
                    act.sem_inc(m_free[bank], 1)
                elif name.startswith("c_sq"):
                    act.wait_ge(ym_done, 8 * b)
                    act.wait_ge(s_x2ld, 16 * b)
                    act.activation(cd[:, h, :], ym[:, h, :], ACT.Square).then_inc(c_sqd, 1)
                elif name.startswith("a_xn"):
                    act.wait_ge(al_n, 2 * t + 2)
                    act.activation(xn[:, h, :], gt[:, h, :], ACT.Identity, scale=col[:, C_G + h:C_G + h + 1],
                                   bias=col[:, C_B + h:C_B + h + 1]).then_inc(xn_done, 1)
                else:
                    own, sq, rs, s_sq, s_var, s_ln, s_rs, s_n, tt = (
                        ("a", sq_a, rs_a, al_sq, al_var, al_ln, al_rs, al_n, t) if name[0] == "a"
                        else ("c", sq_c, rs_c, cl_sq, cl_var, cl_ln, cl_rs, cl_n, b - 1))
                    bank, use = banks(kind, b, (f"{own}_mean{h}", 0))
                    act.wait_ge(m_full[bank], use)
                    act.activation(sq[:], mb[:, bank, :], ACT.Square).then_inc(s_sq, 1)
                    act.wait_ge(s_var, 2 * tt + h + 1)
                    rsqrt(rs[:], rs[:], rs[:], LN_EPS, s_ln, 2 * tt + h + 1, s_rs)

            def scan_operands(b, c, s):
                n16 = 64 * b + 16 * c
                k = BUF_OF_STATE[s]
                if s == 0:
                    act.wait_ge(dt_done, 4 * b + c + 1)
                at_least(act, scanned, 2 * (n16 + last_use(BUF_OF_STATE, s)) + 2)
                act.activation(decay[:, k, :], dt[:, c % 2, :], ACT.Exp, scale=a_neg[:, s:s + 1]).then_inc(decayed, 1)
                at_least(act, hc_done, n16 + s - 1)
                for h in range(2):
                    act.wait_ge(c_full, 2 * n16 + 2 * s + h + 1)
                    act.activation(c_sb[:, s % 2, h * HALF:(h + 1) * HALF], cb[:], ACT.Copy).then_inc(c_copied, 1)
                    yield h

            def turn(kind, b):
                for c in range(NC):
                    for s in range(NS):
                        for h in scan_operands(b, c, s):
                            for name in plan(ACT_SEQ, ACT_BATCH, kind, c, 2 * s + h):
                                do(name, kind, b, c)

            act.preload_act_table_set("natural_log_exp_and_others")
            act.wait_ge(s_w, 16 * 15)
            act.activation(a_neg[:], col[:, C_ALOG:C_ALOG + NS], ACT.Exp)
            for k in range(2):
                last = act.activation(word_n[:, k, :], word_f[:, k, :], ACT.Square, accum_out=wn[:, 0, k:k + 1])
            last.then_inc(su_act, 1)
            act.wait_ge(su_act, 1)
            act.activation(wn[:, 1, :], wn[:, 0, :], ACT.Ln).then_inc(su_act, 1)
            act.wait_ge(su_act, 2)
            act.activation(wn[:, 2, :], wn[:, 1, :], ACT.Exp, scale=-0.5).then_inc(su_act, 1)
            act.wait_ge(su_done, 1)
            for name in ("a_rstd0", "a_affine00", "a_affine01", "a_rn", "a_oht0", "a_oht1",
                         "a_rstd1", "a_affine10", "a_affine11", "a_ln0", "a_ln1", "a_xn0", "a_xn1"):
                do(name, "pro", -1, 0)
            for name in ("prep_xc0", "prep_xc1", "prep_z0", "prep_z1", "prep_sig_x", "prep_sig_z", "prep_hi0",
                         "prep_hi1", "prep_mid", "prep_dt0", "prep_dt1", "prep_dt_exp", "prep_dt_ln"):
                do(name, "pro", -1, NC - 1)
            turn(FIRST, 0)
            with act.Fori(1, NB - 1) as b:
                turn(LOOP, b)
            turn(LAST, NB - 1)
            for name in ("c_sq0", "c_sq1", "c_ln0", "c_ln1"):
                do(name, "tail", NB, 0)

        @block.vector
        def _(dve):
            def chain(sem_, before):
                n = [0]

                def link(ins):
                    n[0] += 1
                    ins.then_inc(sem_, 1)
                    dve.wait_ge(sem_, before + n[0])
                    hold_here(dve)
                return link

            def do(name, kind, b, c):
                m = 4 * b + c + 1
                par = (c + 1) % 2
                t = b + 1
                if name == "post_y":
                    dve.wait_ge(summed, 16 * (m - 1))
                    dve.wait_ge(z_silu, m - 1)
                    at_least(dve, ym_done, 2 * (m - 2))
                    at_least(dve, dt_done, m - 1)
                    dve.scalar_tensor_tensor(out=yy[:], in0=xc[:, par, :], scalar=col[:, C_D:C_D + 1],
                                             in1=yp[:].rearrange("p k t -> p (k t)"), op0=ALU.mult,
                                             op1=ALU.add).then_inc(y_taken, 1)
                    dve.wait_ge(y_taken, m - 1)
                    dve.tensor_tensor(yy[:], yy[:], zz[:, par, :], ALU.mult).then_inc(y_gated, 1)
                elif name.startswith("post_skip"):
                    h = int(name[-1])
                    q = (c - 1) % NC
                    lo = DM * (q % 2)
                    bank, use = banks(kind, b, (f"post_out{h}", c))
                    dve.wait_ge(m_full[bank], use)
                    if c == 1:
                        at_least(dve, cl_d, 2 * b)
                    start = PAD + q % 2 + h * HALF
                    dve.scalar_tensor_tensor(
                        out=ym[lo:lo + DM, q // 2, h * HALF:(h + 1) * HALF],
                        in0=xs[lo:lo + DM, q, start:start + HALF],
                        scalar=col[lo:lo + DM, C_SKIP:C_SKIP + 1], in1=mb[lo:lo + DM, bank, :],
                        op0=ALU.mult, op1=ALU.add).then_inc(ym_done, 1)
                    dve.wait_ge(ym_done, 2 * (m - 2) + h + 1)
                    dve.sem_inc(m_free[bank], 1)
                elif name == "prep_clamp_x":
                    dve.wait_ge(x_pre, 2 * (m + 1))
                    dve.tensor_scalar(e_x[:], e_x[:], E_MAX, None, ALU.min).then_inc(x_clamped, 1)
                elif name == "prep_clamp_z":
                    dve.wait_ge(z_pre, 2 * (m + 1))
                    dve.tensor_scalar(e_z[:], e_z[:], E_MAX, None, ALU.min).then_inc(z_clamped, 1)
                elif name.startswith("prep_rest"):
                    h = int(name[-1])
                    at_least(dve, bc_lo, m)
                    bank, use = banks(kind, b, (f"prep_bc{h}", c))
                    cut = slice(h * HALF, (h + 1) * HALF)
                    dve.wait_ge(bc_hi, 2 * m + h + 1)
                    dve.tensor_tensor(rest[:, cut], mb[0:96, bank, :], bc[:, par, cut],
                                      ALU.subtract).then_inc(bc_rest, 1)
                    dve.wait_ge(bc_rest, 2 * m + h + 1)
                    dve.sem_inc(m_free[bank], 1)
                elif name == "prep_dt":
                    dve.wait_ge(dt_ln, m + 1)
                    link = chain(v_dt, 2 * m)
                    link(dve.scalar_tensor_tensor(out=e_x[:], in0=e_z[:], scalar=1.0, in1=e_x[:],
                                                  op0=ALU.subtract, op1=ALU.subtract))
                    link(dve.tensor_tensor(yy[:], yy[:], e_x[:], ALU.subtract))
                    dve.scalar_tensor_tensor(out=dt[:, par, :], in0=dt[:, par, :], scalar=0.0, in1=yy[:],
                                             op0=ALU.max, op1=ALU.add).then_inc(dt_done, 1)
                elif name.startswith("a_stat"):
                    g, j = int(name[-2]), int(name[-1])
                    if g == 0:
                        dve.wait_ge(s_x, 16 * (t + 1))
                    else:
                        dve.wait_ge(x2_done, t + 1)
                    link = chain(v_stat[g], 6 * t + 3 * j)
                    for h in range(2):
                        last = dve.bn_stats(stats[:, j, h, :], xt[:, j, h * HALF:(h + 1) * HALF])
                    link(last)
                    link(dve.bn_aggr(mv[:, j, :], stats[:, j, :, :]))
                    dve.tensor_copy(gs[:, 0, j:j + 1], mv[:, j, 0:1])
                    link(dve.scalar_tensor_tensor(out=gs[:, 1, j:j + 1], in0=mv[:, j, 0:1], scalar=mv[:, j, 0:1],
                                                  in1=mv[:, j, 1:2], op0=ALU.mult, op1=ALU.add))
                elif name.startswith("a_mom"):
                    g = int(name[-1])
                    bank, use = banks(kind, b, (f"a_group{g}", 0))
                    link = chain(v_mom[g], 3 * t)
                    dve.wait_ge(m_full[bank], use)
                    link(dve.tensor_copy(gm[:].rearrange("p a j -> p (a j)"), mb[:, bank, 0:2 * NJ]))
                    dve.sem_inc(m_free[bank], 1)
                    link(dve.tensor_tensor(gsm[:, 3, :], gm[:, 0, :], gm[:, 0, :], ALU.mult))
                    link(dve.tensor_tensor(gsm[:, 0, :], gm[:, 1, :], gsm[:, 3, :], ALU.subtract))
                elif name.startswith("a_newton"):
                    g = int(name[-1])
                    dve.wait_ge(a_rstd[g], t + 1)
                    link = chain(v_newton[g], 5 * t)
                    link(dve.tensor_tensor(gsm[:, 3, :], gsm[:, 2, :], gsm[:, 2, :], ALU.mult))
                    link(dve.scalar_tensor_tensor(out=gsm[:, 6, :], in0=gsm[:, 0, :], scalar=GN_EPS,
                                                  in1=gsm[:, 3, :], op0=ALU.add, op1=ALU.mult))
                    link(dve.tensor_scalar(gsm[:, 7, :], gsm[:, 6, :], -0.5, 1.5, ALU.mult, ALU.add))
                    link(dve.tensor_tensor(gsm[:, 4, :], gsm[:, 2, :], gsm[:, 7, :], ALU.mult))
                    link(dve.scalar_tensor_tensor(out=gsm[:, 5, :], in0=gm[:, 0, :], scalar=-1.0,
                                                  in1=gsm[:, 4, :], op0=ALU.mult, op1=ALU.mult))
                elif name.startswith("a_pick"):
                    i = int(name[-1])
                    bank, use = banks(kind, b, (f"a_sim{i}0", 0))
                    dve.wait_ge(rn_done, t + 1)
                    dve.wait_ge(m_full[bank], use)
                    at_least(dve, hot_copied, 2 * t + i // 2 - 1)
                    link = chain(v_pick, 4 * (4 * t + i))
                    for k in range(2):
                        last = dve.tensor_scalar(sim[:, k, :], mb[:, bank, k * WORDS:(k + 1) * WORDS],
                                                 rn[:, 2 * i + k:2 * i + k + 1], 1.0, ALU.mult, ALU.subtract)
                    link(last)
                    dve.sem_inc(m_free[bank], 1)
                    for k in range(2):
                        last = dve.max(best[:, k, :], sim[:, k, :])
                    link(last)
                    for k in range(2):
                        dve.max_index(where[:, k, :], best[:, k, :], sim[:, k, :])
                    link(dve.tensor_scalar(close[:], best[:, :, 0], -1.25, None, ALU.is_gt))
                    link(dve.tensor_copy(wheref[:], where[:, :, 0]))
                    for k in range(2):
                        last = dve.tensor_scalar(hot[:, 2 * i + k, :], iot[:], wheref[:, k:k + 1], close[:, k:k + 1],
                                                 ALU.is_equal, ALU.mult)
                    last.then_inc(hot_done, 1)
                elif name.startswith("a_keep"):
                    h = int(name[-1])
                    dve.wait_ge(xg_done, t + 1)
                    bank, use = banks(kind, b, (name, 0))
                    dve.wait_ge(m_full[bank], use)
                    for j in range(NJ):
                        v = gt[:, j, h * HALF:(h + 1) * HALF]
                        last = dve.tensor_tensor(v, v, mb[:, bank, :], ALU.mult)
                    last.then_inc(g_kept, 1)
                    dve.wait_ge(g_kept, 2 * t + h + 1)
                    dve.sem_inc(m_free[bank], 1)
                elif name.startswith("a_mix"):
                    h, j = int(name[-2]), int(name[-1])
                    v = gt[:, j, h * HALF:(h + 1) * HALF]
                    bank, use = banks(kind, b, (name.replace("mix", "word"), 0))
                    dve.wait_ge(m_full[bank], use)
                    dve.tensor_tensor(v, mb[:, bank, :], v, ALU.subtract).then_inc(g_mixed, 1)
                    dve.wait_ge(g_mixed, 4 * t + 2 * h + j + 1)
                    dve.sem_inc(m_free[bank], 1)
                elif name.startswith("c_out"):
                    h, mm = int(name[-2]), int(name[-1])
                    cut = slice(h * HALF, (h + 1) * HALF)
                    dve.wait_ge(s_x2ld, 16 * b)
                    bank, use = banks(kind, b, (name.replace("out", "proj"), 0))
                    dve.wait_ge(m_full[bank], use)
                    dve.scalar_tensor_tensor(out=res[:, mm, cut], in0=mb[:, bank, :], scalar=pb2[:, mm:mm + 1],
                                             in1=res[:, mm, cut], op0=ALU.add, op1=ALU.add).then_inc(res_done, 1)
                    dve.wait_ge(res_done, 4 * (b - 1) + 2 * h + mm + 1)
                    dve.sem_inc(m_free[bank], 1)
                else:
                    h = int(name[-1])
                    own, src, dst, sq, rs, s_sq, s_var, s_d, s_n, tt = (
                        ("a", gt, gt, sq_a, rs_a, al_sq, al_var, al_d, al_n, t) if name[0] == "a"
                        else ("c", ym, cd, sq_c, rs_c, cl_sq, cl_var, cl_d, cl_n, b - 1))
                    bank1, use1 = banks(kind, b, (f"{own}_square{h}", 0))
                    dve.wait_ge(m_full[bank1], use1)
                    dve.wait_ge(s_sq, 2 * tt + h + 1)
                    if own == "a" or h == 1:
                        at_least(dve, s_n, 2 * tt + h)
                    dve.tensor_tensor(rs[:], mb[:, bank1, :], sq[:], ALU.subtract).then_inc(s_var, 1)
                    dve.wait_ge(s_var, 2 * tt + h + 1)
                    dve.sem_inc(m_free[bank1], 1)
                    bank0, use0 = banks(kind, b, (f"{own}_mean{h}", 0))
                    for j in range(NJ):
                        last = dve.tensor_tensor(dst[:, j, h * HALF:(h + 1) * HALF], src[:, j, h * HALF:(h + 1) * HALF],
                                                 mb[:, bank0, :], ALU.subtract)
                    last.then_inc(s_d, 1)
                    dve.wait_ge(s_d, 2 * tt + h + 1)
                    dve.sem_inc(m_free[bank0], 1)

            def multiply(b, c, j):
                h = j % 2
                n32 = 128 * b + 32 * c
                v = bx[:, BANK_OF_STEP[j], :]
                if j == 0:
                    dve.wait_ge(u_done, 4 * b + c + 1)
                dve.wait_ge(b_full, n32 + j + 1)
                dve.tensor_tensor(v, v, u[:, c % 2, h * HALF:(h + 1) * HALF], ALU.mult).then_inc(bx_done, 1)

            def scan(b, c, j):
                s, h = divmod(j, 2)
                n16 = 64 * b + 16 * c
                k = BUF_OF_STATE[s]
                dve.wait_ge(bx_done, 2 * n16 + j + 1)
                if h == 0:
                    dve.wait_ge(decayed, n16 + s + 1)
                    at_least(dve, hc_done, n16 + last_use(BUF_OF_STATE, s) + 1)
                else:
                    dve.wait_ge(scanned, 2 * n16 + j)
                dve.tensor_tensor_scan(state[:, k, h * HALF:(h + 1) * HALF], decay[:, k, h * HALF:(h + 1) * HALF],
                                       bx[:, BANK_OF_STEP[j], :], state[:, k, HALF - 1:HALF] if h else 0.0,
                                       ALU.mult, ALU.add).then_inc(scanned, 1)

            def turn(kind, b):
                for c in range(NC):
                    for s in range(NS):
                        for h in range(2):
                            multiply(b, c, 2 * s + h)
                            if 2 * s + h:
                                scan(b, c, 2 * s + h - 1)
                            for name in plan(DVE_SEQ, DVE_BATCH, kind, c, 2 * s + h):
                                do(name, kind, b, c)
                    scan(b, c, SEQ_STEPS - 1)

            link = chain(su_dve, 0)
            dve.memset(oneb[:], 1.0)
            dve.memset(onef[:], 1.0)
            dve.memset(mean_w[:], 1.0 / CH)
            dve.wait_ge(s_w, 16 * 15)
            for k in range(2):
                dve.tensor_tensor(wtap[:, k, :], w_in_f, taps_f[:, k, :], ALU.mult)
            dve.tensor_scalar(ncb[:], col[:, C_CONVB:C_CONVB + 1], -1.0, None, ALU.mult)
            link(dve.tensor_copy(word_hml[:, 0, :, :], word_f))
            dve.sem_inc(su_pe_ready, 1)
            link(dve.tensor_tensor(word_r, word_f, word_hml[:, 0, :, :], ALU.subtract))
            link(dve.tensor_copy(word_hml[:, 1, :, :], word_r))
            link(dve.tensor_tensor(word_hml[:, 2, :, :], word_r, word_hml[:, 1, :, :], ALU.subtract))
            dve.wait_ge(su_act, 3)
            link(dve.tensor_tensor(wn[:, 3, :], wn[:, 2, :], wn[:, 2, :], ALU.mult))
            link(dve.tensor_tensor(wn[:, 4, :], wn[:, 3, :], wn[:, 0, :], ALU.mult))
            link(dve.tensor_scalar(wn[:, 5, :], wn[:, 4, :], -0.5, 1.5, ALU.mult, ALU.add))
            link(dve.tensor_tensor(wn[:, 6, :], wn[:, 2, :], wn[:, 5, :], ALU.mult))
            link(dve.tensor_scalar(word_q[:, 0, :], word_f[:, 0, :], wn[:, 6, 0:1], None, ALU.mult))
            link(dve.tensor_scalar(word_q[:, 1, :], word_f[:, 1, :], wn[:, 6, 1:2], None, ALU.mult))
            dve.sem_inc(su_words, 1)
            dve.wait_ge(m_full[0], 1)
            link(dve.tensor_copy(wdt[:], mb[:, 0, 0:P]))
            dve.sem_inc(m_free[0], 1)
            dve.wait_ge(m_full[1], 1)
            link(dve.tensor_tensor(pb2[:], mb[:, 1, 0:NJ], col[:, C_PB:C_PB + NJ], ALU.add))
            dve.sem_inc(m_free[1], 1)
            for j in range(NJ):
                link(dve.tensor_scalar(wp[:, j, :], wp[:, j, :], col[:, C_G + j:C_G + j + 1], None, ALU.mult))
            link(dve.tensor_scalar(a_neg[:], a_neg[:], -1.0, None, ALU.mult))
            for i in range(4):
                k, j = divmod(i, 2)
                bank, use = banks("pro", -1, ("word", i))
                dve.wait_ge(m_full[bank], use)
                link(dve.tensor_copy(wordn_t[:, j, k * P:(k + 1) * P], mb[:, bank, 0:P]))
                dve.sem_inc(m_free[bank], 1)
            dve.sem_inc(su_done, 1)

            for name in (["a_stat00", "a_stat01", "a_mom0", "a_newton0"] + [f"a_pick{i}" for i in range(4)]
                         + ["a_keep0", "a_mix00", "a_mix01", "a_keep1", "a_mix10", "a_mix11", "a_stat10", "a_stat11", "a_mom1", "a_newton1", "a_ln0", "a_ln1"]):
                do(name, "pro", -1, 0)
            for name in ("prep_clamp_x", "prep_clamp_z", "prep_rest0", "prep_rest1", "prep_dt"):
                do(name, "pro", -1, NC - 1)
            turn(FIRST, 0)
            with dve.Fori(1, NB - 1) as b:
                turn(LOOP, b)
            turn(LAST, NB - 1)
            for name in ("post_y", "post_skip0", "post_skip1", "c_ln0", "c_ln1", "c_out00", "c_out01", "c_out10", "c_out11"):
                do(name, "tail", NB, 0)

        @block.tensor
        def _(pe):
            def enter(kind, b, key):
                bank, use = banks(kind, b, key)
                at_least(pe, m_free[bank], use - 1)
                return bank

            def do(name, kind, b, c):
                m = 4 * b + c + 1
                cm = (c + 1) % NC
                bm = b + 1 if c == NC - 1 else b
                par = (c + 1) % 2
                t = b + 1
                h = int(name[-1]) if name[-1] in "01" else 0
                cut = slice(h * HALF, (h + 1) * HALF)
                if name.startswith("prep_xc"):
                    pe.wait_ge(s_xs[cm], 32 * (bm + 1))
                    bank = enter(kind, b, (name, c))
                    for k in range(2):
                        first = PAD - 2 * k + h * HALF
                        last = pe.matmul(mb[:, bank, :], wtap[:, k, :], xs[:, cm, first:first + HALF],
                                         start=(k == 0), stop=(k == 1))
                    last.then_inc(m_full[bank], 1)
                elif name.startswith("prep_z"):
                    bank = enter(kind, b, (name, c))
                    pe.matmul(mb[:, bank, :], wz[:], xs[0:DM, cm, PAD + h * HALF:PAD + (h + 1) * HALF],
                              start=True, stop=True).then_inc(m_full[bank], 1)
                elif name.startswith("prep_bc"):
                    pe.wait_ge(x_silu, m + 1)
                    bank = enter(kind, b, (name, c))
                    pe.matmul(mb[0:96, bank, :], wx[:], xc[:, par, cut], start=True, stop=True).then_inc(m_full[bank], 1)
                elif name.startswith("prep_dt"):
                    bank = enter(kind, b, (name, c))
                    pe.matmul(mb[:, bank, :], wdt[:], xc[:, par, cut], start=True, stop=True).then_inc(m_full[bank], 1)
                elif name.startswith("post_out"):
                    pe.wait_ge(y_gated, m - 1)
                    lo = DM * ((c - 1) % 2)
                    bank = enter(kind, b, (name, c))
                    pe.matmul(mb[lo:lo + DM, bank, :], wo[:], yy[:, cut], start=True, stop=True).then_inc(m_full[bank], 1)
                elif name.startswith("a_group"):
                    pe.wait_ge(v_stat[h], 6 * (t + 1))
                    bank = enter(kind, b, (name, 0))
                    pe.matmul(mb[:, bank, 0:2 * NJ], grp[:], gs[:].rearrange("p a j -> p (a j)"),
                              start=True, stop=True).then_inc(m_full[bank], 1)
                elif name == "a_norm":
                    pe.wait_ge(a_sqd[0], NJ * (t + 1))
                    bank = enter(kind, b, (name, 0))
                    for i in range(NT):
                        for j in range(NJ):
                            last = pe.matmul(mb[:, bank, i:i + 1], cd[:, j, i * P:(i + 1) * P], onef[:],
                                             start=(j == 0), stop=(j == NJ - 1))
                    last.then_inc(m_full[bank], 1)
                elif name.startswith("a_sim"):
                    q, k = int(name[-2]), int(name[-1])
                    i = 2 * q + k
                    bank = banks(kind, b, (f"a_sim{q}0", 0))[0]
                    if k == 0:
                        enter(kind, b, (name, 0))
                    for j in range(NJ):
                        last = pe.matmul(mb[:, bank, k * WORDS:(k + 1) * WORDS], gt[:, j, i * P:(i + 1) * P],
                                         wordn_t[:, j, :], start=(j == 0), stop=(j == NJ - 1))
                    if k == 1:
                        last.then_inc(m_full[bank], 1)
                elif name.startswith("a_turn"):
                    q = int(name[-1])
                    pe.wait_ge(hot_done, 4 * t + 2 * q + 2)
                    bank = enter(kind, b, (name, 0))
                    dst = mb[:, bank, :].bitcast(BF16).rearrange("p (k t) -> p k t", k=2)
                    for i in range(4):
                        for k in range(2):
                            last = pe.transpose(dst[:, k, i * P:(i + 1) * P], hot[:, 4 * q + i, k * P:(k + 1) * P],
                                                idb[:])
                    last.then_inc(m_full[bank], 1)
                elif name.startswith("a_keep"):
                    h = int(name[-1])
                    pe.wait_ge(hot_copied, 2 * t + h + 1)
                    bank = enter(kind, b, (name, 0))
                    for k in range(2):
                        last = pe.matmul(mb[:, bank, :], oneb[:], hot_t[:, k, h * HALF:(h + 1) * HALF],
                                         start=(k == 0), stop=(k == 1))
                    last.then_inc(m_full[bank], 1)
                elif name.startswith("a_word"):
                    h, j = int(name[-2]), int(name[-1])
                    bank = enter(kind, b, (name, 0))
                    for i in range(6):
                        part, k = divmod(i, 2)
                        last = pe.matmul(mb[:, bank, :], word_hml[:, part, k, j * P:(j + 1) * P],
                                         hot_t[:, k, h * HALF:(h + 1) * HALF], start=(i == 0), stop=(i == 5))
                    last.then_inc(m_full[bank], 1)
                elif name.startswith("c_proj"):
                    h, mm = int(name[-2]), int(name[-1])
                    pe.wait_ge(cl_n, 2 * (b - 1) + h + 1)
                    bank = enter(kind, b, (name, 0))
                    for j in range(NJ):
                        last = pe.matmul(mb[:, bank, :], wp[:, j, mm * P:(mm + 1) * P],
                                         cd[:, j, h * HALF:(h + 1) * HALF], start=(j == 0), stop=(j == NJ - 1))
                    last.then_inc(m_full[bank], 1)
                else:
                    if name[0] == "a":
                        pe.wait_ge(a_sqd[1], NJ * (t + 1))
                        tile = gt if "mean" in name else xn
                    else:
                        pe.wait_ge(c_sqd, NJ * b)
                        tile = ym if "mean" in name else cd
                    bank = enter(kind, b, (name, 0))
                    for j in range(NJ):
                        last = pe.matmul(mb[:, bank, :], mean_w[:], tile[:, j, cut], start=(j == 0),
                                         stop=(j == NJ - 1))
                    last.then_inc(m_full[bank], 1)

            def broadcast(b, c, j):
                s, h = divmod(j, 2)
                n32 = 128 * b + 32 * c
                cut = slice(h * HALF, (h + 1) * HALF)
                if j == 0:
                    pe.wait_ge(bc_lo, 4 * b + c + 1)
                at_least(pe, scanned, n32 + last_use(BANK_OF_STEP, j) + 1)
                pe.matmul(bx[:, BANK_OF_STEP[j], :], sel[:, s, :], bc[:, c % 2, cut], start=True,
                          stop=True).then_inc(b_full, 1)
                at_least(pe, c_copied, n32 + j)
                pe.matmul(cb[:], sel[:, NS + s, :], bc[:, c % 2, cut], start=True, stop=True).then_inc(c_full, 1)

            def sum_states(b, c, r):
                s, h = divmod(r, 2)
                n16 = 64 * b + 16 * c
                if r == 0:
                    at_least(pe, y_taken, 4 * b + c)
                pe.wait_ge(hc_done, n16 + s + 1)
                last = pe.matmul(yp[:, h, :], idf[:], hc[:, BUF_OF_STATE[s], h * HALF:(h + 1) * HALF],
                                 start=(s == 0), stop=(s == NS - 1))
                if h == 1:
                    last.then_inc(summed, 1)

            def turn(kind, b):
                for c in range(NC):
                    for j in range(SEQ_STEPS):
                        broadcast(b, c, j)
                        for r in range(SEQ_STEPS):
                            if SUM_AT[r] == j:
                                sum_states(b, c, r)
                            elif SUM_AT[r] == j + SEQ_STEPS and not (kind == FIRST and c == 0):
                                sum_states(b if c else b - 1, (c - 1) % NC, r)
                        for name in plan(PE_SEQ, PE_BATCH, kind, c, j):
                            do(name, kind, b, c)

            pe.wait_ge(s_w, 16 * 15)
            pe.wait_ge(su_pe_ready, 1)
            pe.matmul(mb[:, 0, 0:P], wdt4[:, 1, :], wdt4[:, 0, :], start=True, stop=True).then_inc(m_full[0], 1)
            for mm in range(NJ):
                for j in range(NJ):
                    last = pe.matmul(mb[:, 1, mm:mm + 1], wp[:, j, mm * P:(mm + 1) * P], col[:, C_B + j:C_B + j + 1],
                                     start=(j == 0), stop=(j == NJ - 1))
            last.then_inc(m_full[1], 1)
            pe.wait_ge(su_words, 1)
            for i in range(4):
                k, j = divmod(i, 2)
                bank = enter("pro", -1, ("word", i))
                pe.transpose(mb[:, bank, 0:P], word_q[:, k, j * P:(j + 1) * P], idf[:]).then_inc(m_full[bank], 1)
            pe.wait_ge(su_done, 1)
            for name in A_ALL:
                do(name, "pro", -1, 0)
            for name in PREP_ALL:
                do(name, "pro", -1, NC - 1)
            turn(FIRST, 0)
            with pe.Fori(1, NB - 1) as b:
                turn(LOOP, b)
            turn(LAST, NB - 1)
            for r in range(SEQ_STEPS):
                if SUM_AT[r] >= SEQ_STEPS:
                    sum_states(NB - 1, NC - 1, r)
            for name in ["post_out0", "post_out1"] + C_STATS + C_PROJ:
                do(name, "tail", NB, 0)


def kernel(**inputs):
    import ml_dtypes
    import numpy as np
    import concourse.bacc as _bacc
    from concourse.bass_utils import run_bass_kernel_spmd as _run

    g = {k.replace("L1_conv_", ""): np.asarray(v) for k, v in inputs.items()}
    x_proj = g["x_proj_w"]
    cols = np.concatenate([
        g["conv_b"].reshape(P, 1), g["dt_proj_b"].reshape(P, 1), g["D_param"].reshape(P, 1), g["A_log"],
        g["norm_g"].reshape(NJ, P).T, g["norm_b"].reshape(NJ, P).T, g["proj_b"].reshape(NJ, P).T,
        np.broadcast_to(g["skip_scale"].reshape(1, 1), (P, 1))], axis=1)
    w_in_t = g["in_proj_w"][:P].T
    taps = g["conv_w"].T
    w_taps = np.empty((P, 2, P), taps.dtype)
    for k in range(2):
        w_taps[:DM, k] = taps[3 - 2 * k]
        w_taps[DM:, k] = taps[2 - 2 * k]
    select = np.zeros((96, 2 * NS, P), ml_dtypes.bfloat16)
    for r in range(96):
        select[r, r % 32] = 1
    arrays = {
        "x": g["x"], "words": g["L0_conv_negative_dict"], "cols": cols,
        "w_in": np.concatenate([w_in_t, w_in_t], axis=0), "w_z": g["in_proj_w"][P:].T, "w_taps": w_taps,
        "w_x": np.concatenate([x_proj[4:].T] * 3, axis=1), "w_dt": g["dt_proj_w"].T, "w_xdt": x_proj[:4],
        "w_out": g["out_proj_w"].T, "w_proj": g["proj_w"].T,
        "iota": np.broadcast_to(np.arange(WORDS, dtype=np.float32), (P, WORDS)),
        "ident_f": np.eye(P, dtype=np.float32), "ident_b": np.eye(P, dtype=ml_dtypes.bfloat16),
        "group_mean": np.kron(np.eye(P // 8, dtype=np.float32), np.full((8, 8), 0.125, np.float32)),
        "select": select,
    }
    nc = _bacc.Bacc("TRN2", target_bir_lowering=False, num_devices=1)
    named, args = {}, []
    for name, a in arrays.items():
        a = np.ascontiguousarray(a)
        named[f"in_{name}"] = a
        args.append(nc.dram_tensor(f"in_{name}", a.shape, mybir.dt.from_np(a.dtype), kind="ExternalInput").ap())
    out = nc.dram_tensor("out", (NB, CH, 32, 32), F32, kind="ExternalOutput").ap()
    build(nc, *args, out)
    r = _run(nc, [named], core_ids=[0])
    return r.results[0]["out"]
```

```python
from contextlib import ExitStack

import concourse.bass as bass
from concourse import mybir

ALU = mybir.AluOpType
ACT = mybir.ActivationFunctionType
F32 = mybir.dt.float32
BF16 = mybir.dt.bfloat16
U32 = mybir.dt.uint32

P = 128
NB = 16
CH = 256
NJ = CH // P
L = 1024
HALF = 512
NC = 4
DM = CH // NC
NS = 16
SEQ_STEPS = 2 * NS
NT = L // P
WORDS = 256
PAD = 3
LN_EPS = 1e-5
GN_EPS = 1e-5
E_MAX = float(2.0 ** 60)

C_CONVB, C_DTB, C_D, C_ALOG, C_G, C_B, C_PB, C_SKIP, N_COLS = 0, 1, 2, 3, 19, 21, 23, 25, 26

BUF_OF_STATE = [0, 1, 2] * 5 + [1]


def last_use(order, i):
    d = 1
    while order[(i - d) % len(order)] != order[i]:
        d += 1
    return i - d


def at_least(eng, sem, value):
    if isinstance(value, int) and value <= 0:
        return
    eng.wait_ge(sem, value)


PE_SEQ = {7: ["prep_xc0"], 9: ["prep_xc1"], 11: ["prep_z0"], 12: ["prep_z1"], 13: ["post_out0"],
          14: ["post_out1"], 17: ["prep_bc0"], 18: ["prep_bc1"], 20: ["prep_dt0"], 21: ["prep_dt1"]}
ACT_SEQ = {8: ["prep_xc0"], 10: ["prep_xc1"], 12: ["prep_z0"], 13: ["prep_z1"], 14: ["prep_sig_x"],
           16: ["prep_sig_z"], 17: ["prep_hi0"], 18: ["prep_hi1"], 21: ["prep_dt0"], 22: ["prep_dt1"],
           20: ["prep_mid"], 23: ["prep_dt_exp"], 24: ["prep_dt_one"], 25: ["prep_dt_ln"]}
DVE_SEQ = {4: ["post_y0"], 5: ["post_y1"], 7: ["post_gate0"], 8: ["post_gate1"], 11: ["prep_clamp_x"],
           14: ["prep_clamp_z", "post_skip0"], 15: ["post_skip1"],
           18: ["prep_rest0"], 19: ["prep_rest1"], 26: ["prep_dt_err"], 27: ["prep_dt_log"], 28: ["prep_dt_sum"]}
POOL_SEQ = {12: ["prep_silu_x"], 14: ["prep_silu_z"], 22: ["prep_lo"], 26: ["prep_u"]}
PE_BATCH = {(0, 3): ["a_group0"], (0, 15): ["a_norm0"], (0, 16): ["a_norm1"], (0, 22): ["a_sim00"], (0, 23): ["a_sim01"],
            (0, 24): ["a_sim10"], (0, 25): ["a_sim11"], (0, 27): ["a_sim20"], (0, 28): ["a_sim21"],
            (0, 30): ["a_sim30"], (0, 31): ["a_sim31"],
            (1, 0): ["c_mean0"], (1, 2): ["c_square0"], (1, 4): ["c_mean1"], (1, 5): ["c_square1"],
            (1, 15): ["c_proj00"], (1, 16): ["c_proj01"],
            (1, 22): ["a_turn0"], (1, 23): ["a_turn1"],
            (1, 25): ["a_keep0"], (1, 27): ["a_word00"], (1, 28): ["a_word01"], (1, 29): ["a_keep1"],
            (1, 30): ["a_word10"], (1, 31): ["a_word11"], (2, 8): ["a_group1"],
            (2, 15): ["c_proj10"], (2, 16): ["c_proj11"],
            (2, 23): ["a_mean0"], (2, 24): ["a_square0"], (2, 28): ["a_mean1"], (2, 29): ["a_square1"]}
ACT_BATCH = {(0, 5): ["a_rstd0"], (0, 7): ["a_affine00"], (0, 9): ["a_affine01"], (0, 16): ["a_rn"],
             (0, 28): ["c_sq0"], (0, 30): ["c_sq1"],
             (1, 1): ["c_msq0"], (1, 4): ["c_rs0"], (1, 5): ["c_msq1"], (1, 7): ["c_rs1"],
             (1, 23): ["a_oht0"], (1, 24): ["a_oht1"],
             (2, 10): ["a_rstd1"], (2, 11): ["a_affine10"], (2, 15): ["a_affine11"], (2, 24): ["a_msq0"],
             (2, 27): ["a_rs0"], (2, 29): ["a_msq1"], (2, 31): ["a_rs1"], (3, 2): ["a_xn0"], (3, 3): ["a_xn1"]}
DVE_BATCH = {(0, 0): ["a_stat00"], (0, 2): ["a_stat01"], (0, 4): ["a_mom0"], (0, 6): ["a_newton0"],
             (0, 24): ["a_pick0"], (0, 25): ["a_hot0"], (0, 26): ["a_pick1"], (0, 30): ["a_hot1"],
             (0, 31): ["a_pick2"], (1, 0): ["a_hot2"], (1, 1): ["a_pick3"],
             (1, 3): ["c_var0", "c_ctr0"], (1, 6): ["c_var1", "c_ctr1"], (1, 9): ["a_hot3"],
             (1, 16): ["c_out00"], (1, 17): ["c_out01"], (2, 16): ["c_out10"], (2, 17): ["c_out11"],
             (1, 26): ["a_keep0"], (1, 28): ["a_mix00"], (1, 29): ["a_mix01"], (1, 30): ["a_keep1"],
             (1, 31): ["a_mix10"], (2, 0): ["a_mix11"], (2, 5): ["a_stat10"], (2, 6): ["a_stat11"],
             (2, 8): ["a_mom1"], (2, 10): ["a_newton1"],
             (2, 25): ["a_var0"], (2, 26): ["a_ctr0"], (2, 30): ["a_var1"], (2, 31): ["a_ctr1"]}
POOL_BATCH = {(0, 8): ["a_squares"], (0, 16): ["a_xg0"], (0, 18): ["a_xg1"], (1, 4): ["c_scale0"], (1, 8): ["c_scale1"],
              (2, 0): ["a_x20"], (2, 2): ["a_x21"], (2, 26): ["a_scale0"], (2, 30): ["a_scale1"]}
SP_BATCH = {(0, 0): ["x_in", "x2_back"], (0, 5): ["xs3"], (2, 4): ["x2_store"],
            (2, 18): ["out"], (3, 4): ["xs0", "xs1", "xs2"]}
SUM_AT = [7 + r - (r >= 13) - (r >= 21) for r in range(SEQ_STEPS)]

FIRST, LOOP, LAST = "first", "loop", "last"


def plan(seq_plan, batch_plan, kind, c, j):
    names = []
    for name in seq_plan.get(j, []):
        if name.startswith("post") and kind == FIRST and c == 0:
            continue
        if name.startswith("prep") and kind == LAST and c == NC - 1:
            continue
        names.append(name)
    for name in batch_plan.get((c, j), []):
        if kind == FIRST and (name in ("x2_back", "out") or name.startswith("c_")):
            continue
        if kind == LAST and (name.startswith("a_") or name in ("x_in", "x2_store", "xs0", "xs1", "xs2")):
            continue
        names.append(name)
    return names


SINGLE = {"a_group0": 0, "a_norm0": 1, "a_sim00": 0, "a_sim10": 1, "a_sim20": 0, "a_sim30": 1,
          "a_turn0": 0, "a_turn1": 1, "a_keep0": 0, "a_word00": 1, "a_word01": 0, "a_keep1": 1,
          "a_word10": 0, "a_word11": 1, "a_group1": 1}


def bank_use(name, c):
    if name.startswith(("prep", "post")):
        return [(int(name[-1]), (name, c))]
    if name in SINGLE:
        return [(SINGLE[name], (name, 0))]
    if name.startswith("a_sim") or name == "a_norm1":
        return []
    if name.startswith("c_proj"):
        return [(int(name[-1]), (name, 0))]
    return [(0 if "mean" in name else 1, (name, 0))]


SETUP_USES = [(0, "dtw"), (1, "pb")] + [(i % 2, ("word", i)) for i in range(4)]
STATS = ["mean0", "square0", "mean1", "square1"]
A_ALL = (["a_group0", "a_norm0", "a_norm1"] + [f"a_sim{i}{k}" for i in range(4) for k in range(2)]
         + ["a_turn0", "a_turn1", "a_keep0", "a_word00", "a_word01", "a_keep1", "a_word10", "a_word11", "a_group1"]
         + ["a_" + w for w in STATS])
PREP_ALL = [f"prep_{w}{h}" for w in ("xc", "z", "bc", "dt") for h in range(2)]
C_STATS = ["c_" + w for w in STATS]
C_PROJ = [f"c_proj{h}{m}" for h in range(2) for m in range(NJ)]


class Banks:

    def __init__(self):
        self.at, self.count = {}, {}
        self.note("pro", SETUP_USES + [u for n in A_ALL for u in bank_use(n, 0)]
                  + [u for n in PREP_ALL for u in bank_use(n, NC - 1)])
        for kind in (FIRST, LOOP, LAST):
            self.note(kind, [u for c in range(NC) for j in range(SEQ_STEPS)
                             for n in plan(PE_SEQ, PE_BATCH, kind, c, j) for u in bank_use(n, c)])
        self.note("tail", [u for n in ["post_out0", "post_out1"] + C_STATS + C_PROJ for u in bank_use(n, 0)])

    def note(self, kind, uses):
        n = [0, 0]
        for bank, key in uses:
            self.at[kind, key] = (bank, n[bank])
            n[bank] += 1
        self.count[kind] = n

    def __call__(self, kind, b, key):
        bank, place = self.at[kind, key]
        before = 0
        if kind != "pro":
            before = self.count["pro"][bank]
        if kind in (LOOP, LAST, "tail"):
            before += self.count[FIRST][bank]
        if kind == LOOP:
            before = self.count[LOOP][bank] * (b - 1) + before
        if kind in (LAST, "tail"):
            before += self.count[LOOP][bank] * (NB - 2)
        if kind == "tail":
            before += self.count[LAST][bank]
        return bank, before + place + 1


def build(nc, x, words, cols, w_in, w_z, w_taps, w_x, w_dt, w_xdt, w_out, w_proj,
          iota, ident_f, ident_b, group_mean, select, out):
    x_v = x.rearrange("b (j p) h w -> b p j (h w)", p=P)
    out_v = out.rearrange("b (j p) h w -> b p j (h w)", p=P)
    x2_v = nc.dram_tensor("x2_scratch", (NB, P, NJ, L), F32).ap()
    banks = Banks()

    with ExitStack() as ctx:
        def sb(name, shape, dt=F32):
            return ctx.enter_context(nc.sbuf_tensor(name, shape, dt))

        def ps(name, shape):
            return ctx.enter_context(nc.psum_tensor(name, shape, F32))

        def sem(name):
            return ctx.enter_context(nc.semaphore(name))

        bb = ps("bb", [P, 2, HALF])
        cb = ps("cb", [P, 2, HALF])
        yp = ps("yp", [P, 2, HALF])
        mb = ps("mb", [P, 2, HALF])

        dt = sb("dt", [P, 2, L])
        u = sb("u", [P, 2, L])
        xc = sb("xc", [P, 2, L])
        zz = sb("zz", [P, 2, L])
        bc = sb("bc", [96, 2, L], BF16)
        bx = sb("bx", [P, 2, L])
        decay = sb("decay", [P, 3, L])
        c_sb = sb("c_sb", [P, 2, L])
        state = sb("state", [P, 3, L])
        hc = sb("hc", [P, 3, L])
        xs = sb("xs", [P, NC, L + PAD + 1])
        e_x = sb("e_x", [P, L])
        e_z = sb("e_z", [P, L])
        rest = sb("rest", [96, L])
        yy = sb("yy", [P, L])
        ym = sb("ym", [P, NJ, L])
        cd = sb("cd", [P, NJ, L])
        res = sb("res", [P, NJ, L])
        xt = sb("xt", [P, NJ, L])
        gt = sb("gt", [P, NJ, L])
        xn = sb("xn", [P, NJ, L])
        hot_t = sb("hot_t", [P, 2, L], BF16)
        sim = sb("sim", [P, 2, WORDS])
        best = sb("best", [P, 2, 8])
        where = sb("where", [P, 2, 8], U32)
        wheref = sb("wheref", [P, 2])
        close = sb("close", [P, 2])
        hot = sb("hot", [P, NT, WORDS], BF16)
        rn_l = sb("rn_l", [P, NT])
        rn = sb("rn", [P, NT])
        stats = sb("stats", [P, NJ, 2, 6])
        mv = sb("mv", [P, NJ, 2])
        gs = sb("gs", [P, 2, NJ])
        gm = sb("gm", [P, 2, NJ])
        gsm = sb("gsm", [P, 8, NJ])
        sq = sb("sq", [P, HALF])
        rs = sb("rs", [P, 2, HALF])
        col = sb("col", [P, N_COLS])
        a_neg = sb("a_neg", [P, NS])
        ncb = sb("ncb", [P, 1])
        pb2 = sb("pb2", [P, NJ])
        wtap = sb("wtap", [P, 2, P])
        wz = sb("wz", [DM, P])
        wx = sb("wx", [P, 96])
        wdt4 = sb("wdt4", [4, 2, P])
        wdt = sb("wdt", [P, P])
        wo = sb("wo", [P, DM])
        wp = sb("wp", [P, NJ, CH])
        idf = sb("idf", [P, P])
        idb = sb("idb", [P, P], BF16)
        oneb = sb("oneb", [P, P], BF16)
        mean_w = sb("mean_w", [P, P])
        onef = sb("onef", [P, 1])
        grp = sb("grp", [P, P])
        sel = sb("sel", [96, 2 * NS, P], BF16)
        iot = sb("iot", [P, WORDS])
        word_hml = sb("word_hml", [P, 3, 2, CH], BF16)
        wordn_t = sb("wordn_t", [P, NJ, WORDS])
        wn = sb("wn", [P, 8, 2])
        word_f = cd[:, 0, 0:512].rearrange("p (k c) -> p k c", k=2)
        word_n = cd[:, 1, 0:512].rearrange("p (k c) -> p k c", k=2)
        word_r = res[:, 0, 0:512].rearrange("p (k c) -> p k c", k=2)
        word_q = res[:, 1, 0:512].rearrange("p (k c) -> p k c", k=2)
        w_in_f = ym[:, 0, 0:P]
        taps_f = ym[:, 0, P:3 * P].rearrange("p (k d) -> p k d", k=2)

        s_w = sem("weights_in")
        s_x = sem("x_in")
        s_xs = [sem(f"xs_in{c}") for c in range(NC)]
        s_x2st = sem("x2_stored")
        s_x2ld = sem("x2_back")
        s_out = sem("out_stored")
        m_full = [sem(f"shared_full{i}") for i in range(2)]
        m_free = [sem(f"shared_free{i}") for i in range(2)]
        b_full = sem("b_broadcast")
        bx_done = sem("bx_multiplied")
        scanned = sem("scanned")
        decayed = sem("decay_ready")
        c_full = sem("c_broadcast")
        c_copied = sem("c_copied")
        hc_done = sem("hc_ready")
        summed = sem("y_summed")
        y_taken = sem("y_taken")
        y_gated = sem("y_gated")
        x_pre = sem("x_pre")
        x_clamped = sem("x_clamped")
        x_ln = sem("x_ln")
        x_sig = sem("x_sig")
        x_silu = sem("x_silu")
        z_pre = sem("z_pre")
        z_clamped = sem("z_clamped")
        z_ln = sem("z_ln")
        z_sig = sem("z_sig")
        z_silu = sem("z_silu")
        bc_hi = sem("bc_hi")
        bc_mid = sem("bc_mid")
        bc_lo = sem("bc_lo")
        dt_abs = sem("dt_abs")
        dt_exp = sem("dt_exp")
        v_dt = sem("dve_softplus")
        dt_one = sem("dt_exp_plus_one")
        dt_ln = sem("dt_ln")
        dt_done = sem("dt_ready")
        u_done = sem("u_ready")
        v_stat = [sem(f"dve_stat{g}") for g in range(2)]
        v_mom = [sem(f"dve_moments{g}") for g in range(2)]
        v_newton = [sem(f"dve_newton{g}") for g in range(2)]
        a_rln = [sem(f"rstd_ln{g}") for g in range(2)]
        a_rstd = [sem(f"rstd_guess{g}") for g in range(2)]
        a_aff = [sem(f"normalised{g}") for g in range(2)]
        a_sqd = [sem(f"squared{g}") for g in range(2)]
        sq_added = sem("squares_added")
        xg_done = sem("x_plus_g")
        rn_ln = sem("pixel_norm_ln")
        rn_done = sem("pixel_norm")
        v_pick = sem("dve_pick")
        hot_done = sem("one_hot_ready")
        hot_copied = sem("one_hot_turned")
        x2_done = sem("x2_ready")
        al_sq, cl_sq = sem("a_mean_squared"), sem("c_mean_squared")
        al_ln, cl_ln = sem("a_variance_ln"), sem("c_variance_ln")
        al_rs, cl_rs = sem("a_rstd"), sem("c_rstd")
        al_n, cl_n = sem("a_scaled"), sem("c_scaled")
        xn_done = sem("xn_ready")
        c_sqd = sem("ym_squared")
        su_mem = sem("setup_memset")
        su_dve = sem("setup_dve")
        su_act = sem("setup_act")
        su_pe_ready = sem("setup_for_pe")
        su_words = sem("setup_words")
        su_done = sem("setup_done")

        passed = sem("passed")

        def hold_here(eng):
            eng.sem_inc(passed, 1)

        block = ctx.enter_context(nc.Block())

        @block.sync
        def _(sp):
            def await_(sem_, value):
                if not isinstance(value, int) or value > 0:
                    sp.wait_ge(sem_, value)
                    hold_here(sp)

            loads = [(col[:], cols), (word_f, words.rearrange("(k p) c -> p k c", p=P)), (w_in_f, w_in),
                     (taps_f, w_taps), (wz[:], w_z), (wx[:], w_x), (wdt4[:, 0, :], w_dt), (wdt4[:, 1, :], w_xdt),
                     (wo[:], w_out), (wp[:], w_proj.rearrange("(j p) o -> p j o", p=P)), (idf[:], ident_f),
                     (idb[:], ident_b), (grp[:], group_mean), (sel[:], select), (iot[:], iota)]
            sp.dma_start(xt[:], x_v[0]).then_inc(s_x, 16)
            for dst, src in loads:
                sp.dma_start(dst, src).then_inc(s_w, 16)

            def load_chunk(c, t, kind, b):
                await_(xn_done, NJ * t + c // 2 + 1)
                after = (c + 1) % NC
                if kind != "pro" and not (kind == FIRST and after == 0):
                    for q in range(2):
                        bank, use = banks(kind, b, (f"post_out{q}", after))
                        await_(m_free[bank], use)
                src = xn[DM * (c % 2):DM * (c % 2) + DM, c // 2, :]
                sp.dma_start(xs[0:DM, c, PAD:PAD + L], src).then_inc(s_xs[c], 16)
                sp.dma_start(xs[DM:P, c, PAD + 1:PAD + 1 + L], src).then_inc(s_xs[c], 16)

            def store_x2(t):
                await_(x2_done, NJ * (t + 1))
                sp.dma_start(x2_v[t], xt[:]).then_inc(s_x2st, 16)

            def do(name, kind, b):
                t = b + 1
                if name == "x2_back":
                    await_(s_x2st, 16 * b)
                    sp.dma_start(res[:], x2_v[b - 1]).then_inc(s_x2ld, 16)
                elif name == "out":
                    for q in range(2):
                        bank, use = banks(kind, b, (f"c_proj1{q}", 0))
                        await_(m_free[bank], use)
                    sp.dma_start(out_v[b - 1], res[:]).then_inc(s_out, 16)
                    await_(s_out, 16 * b)
                elif name == "x_in":
                    await_(a_sqd[1], NJ * t)
                    await_(s_x2st, 16 * t)
                    sp.dma_start(xt[:], x_v[t]).then_inc(s_x, 16)
                elif name == "x2_store":
                    store_x2(b + 1)
                elif name == "xs3":
                    load_chunk(3, b, kind, b)
                else:
                    load_chunk(int(name[-1]), b + 1, kind, b)

            def turn(kind, b):
                for c in range(NC):
                    for j in range(SEQ_STEPS):
                        for name in plan({}, SP_BATCH, kind, c, j):
                            do(name, kind, b)

            store_x2(0)
            await_(su_mem, 1)
            for c in range(3):
                load_chunk(c, 0, "pro", -1)
            turn(FIRST, 0)
            with sp.Fori(1, NB - 1) as b:
                turn(LOOP, b)
            turn(LAST, NB - 1)
            do("x2_back", "tail", NB)
            do("out", "tail", NB)

        @block.gpsimd
        def _(pool):
            def do(name, kind, b, c, s=-1):
                m = 4 * b + c + 1
                par = (c + 1) % 2
                if name == "prep_silu_x":
                    pool.wait_ge(x_sig, m + 1)
                    pool.tensor_tensor(xc[:, par, :], xc[:, par, :], e_x[:], ALU.mult).then_inc(x_silu, 1)
                elif name == "prep_silu_z":
                    pool.wait_ge(z_sig, m + 1)
                    pool.tensor_tensor(zz[:, par, :], zz[:, par, :], e_z[:], ALU.mult).then_inc(z_silu, 1)
                elif name == "prep_lo":
                    pool.wait_ge(bc_mid, m + 1)
                    pool.wait_ge(z_silu, m + 1)
                    at_least(pool, hc_done, 16 * m - NS + s + 1)
                    pool.tensor_tensor(bc[64:96, par, :], rest[64:96, :], bc[64:96, par, :],
                                       ALU.subtract).then_inc(bc_lo, 1)
                    pool.wait_ge(bc_lo, m + 1)
                elif name == "prep_u":
                    pool.wait_ge(dt_done, m + 1)
                    at_least(pool, bx_done, 32 * (m - 1))
                    pool.tensor_tensor(u[:, par, :], dt[:, par, :], xc[:, par, :], ALU.mult).then_inc(u_done, 1)
                elif name == "a_squares":
                    pool.wait_ge(a_sqd[0], NJ * (b + 2))
                    pool.tensor_tensor(cd[:, 0, :], cd[:, 0, :], cd[:, 1, :], ALU.add).then_inc(sq_added, 1)
                elif name.startswith("a_xg"):
                    j = int(name[-1])
                    pool.wait_ge(a_sqd[0], NJ * (b + 2))
                    pool.tensor_tensor(xt[:, j, :], xt[:, j, :], gt[:, j, :], ALU.add).then_inc(xg_done, 1)
                elif name.startswith("a_x2"):
                    j = int(name[-1])
                    pool.wait_ge(xg_done, NJ * (b + 2))
                    for h in range(2):
                        bank, use = banks(kind, b, (f"a_word{h}{j}", 0))
                        pool.wait_ge(m_free[bank], use)
                    pool.tensor_tensor(xt[:, j, :], xt[:, j, :], gt[:, j, :], ALU.add).then_inc(x2_done, 1)
                else:
                    h = int(name[-1])
                    tile, own, s_rs, done, t = ((gt, "a", al_rs, al_n, b + 1) if name[0] == "a"
                                                else (cd, "c", cl_rs, cl_n, b - 1))
                    pool.wait_ge(s_rs, 2 * t + h + 1)
                    bank, use = banks(kind, b, (f"{own}_mean{h}", 0))
                    pool.wait_ge(m_free[bank], use)
                    for j in range(NJ):
                        v = tile[:, j, h * HALF:(h + 1) * HALF]
                        last = pool.tensor_tensor(v, v, rs[:, h, :], ALU.mult)
                    last.then_inc(done, 1)

            def gate(b, c, s):
                n16 = 64 * b + 16 * c
                k = BUF_OF_STATE[s]
                pool.wait_ge(scanned, n16 + s + 1)
                pool.wait_ge(c_copied, 2 * n16 + 2 * s + 2)
                at_least(pool, summed, 2 * (n16 + last_use(BUF_OF_STATE, s) + 1))
                pool.tensor_tensor(hc[:, k, :], state[:, k, :], c_sb[:, s % 2, :], ALU.mult).then_inc(hc_done, 1)

            def turn(kind, b):
                for c in range(NC):
                    for s in range(NS):
                        gate(b, c, s)
                        for h in range(2):
                            for name in plan(POOL_SEQ, POOL_BATCH, kind, c, 2 * s + h):
                                do(name, kind, b, c, s)

            pool.memset(xs[:, :, 0:PAD + 1], 0.0).then_inc(su_mem, 1)
            for name in ("a_squares", "a_xg0", "a_xg1", "a_x20", "a_x21", "a_scale0", "a_scale1"):
                do(name, "pro", -1, 0)
            for name in ("prep_silu_x", "prep_silu_z", "prep_lo", "prep_u"):
                do(name, "pro", -1, NC - 1)
            turn(FIRST, 0)
            with pool.Fori(1, NB - 1) as b:
                turn(LOOP, b)
            turn(LAST, NB - 1)
            do("c_scale0", "tail", NB, 0)
            do("c_scale1", "tail", NB, 0)

        @block.scalar
        def _(act):
            def rsqrt(dst, tmp, src, eps, ln_done, ln_count, done):
                act.activation(tmp, src, ACT.Ln, bias=eps).then_inc(ln_done, 1)
                act.wait_ge(ln_done, ln_count)
                return act.activation(dst, tmp, ACT.Exp, scale=-0.5).then_inc(done, 1)

            def sigmoid(e, clamped, ln_done, done, m):
                act.wait_ge(clamped, m + 1)
                act.activation(e, e, ACT.Ln, bias=1.0).then_inc(ln_done, 1)
                act.wait_ge(ln_done, m + 1)
                act.activation(e, e, ACT.Exp, scale=-1.0).then_inc(done, 1)

            def do(name, kind, b, c):
                m = 4 * b + c + 1
                par = (c + 1) % 2
                t = b + 1
                h = int(name[-1]) if name[-1] in "01" else 0
                cut = slice(h * HALF, (h + 1) * HALF)
                if name.startswith("prep_xc"):
                    at_least(act, u_done, m)
                    at_least(act, dt_done, m)
                    at_least(act, y_taken, 2 * (m - 1))
                    bank, use = banks(kind, b, (name, c))
                    act.wait_ge(m_full[bank], use)
                    act.activation(e_x[:, cut], mb[:, bank, :], ACT.Exp, bias=ncb[:, 0:1], scale=-1.0).then_inc(x_pre, 1)
                    act.activation(xc[:, par, cut], mb[:, bank, :], ACT.Identity,
                                   bias=col[:, C_CONVB:C_CONVB + 1]).then_inc(m_free[bank], 1)
                elif name.startswith("prep_z"):
                    at_least(act, dt_done, m)
                    at_least(act, y_gated, 2 * (m - 1))
                    bank, use = banks(kind, b, (name, c))
                    act.wait_ge(m_full[bank], use)
                    act.activation(e_z[:, cut], mb[:, bank, :], ACT.Exp, scale=-1.0).then_inc(z_pre, 1)
                    act.activation(zz[:, par, cut], mb[:, bank, :], ACT.Copy).then_inc(m_free[bank], 1)
                elif name == "prep_sig_x":
                    sigmoid(e_x[:], x_clamped, x_ln, x_sig, m)
                elif name == "prep_sig_z":
                    sigmoid(e_z[:], z_clamped, z_ln, z_sig, m)
                elif name.startswith("prep_hi"):
                    at_least(act, b_full, 32 * (m - 1))
                    at_least(act, c_full, 32 * (m - 1))
                    bank, use = banks(kind, b, (f"prep_bc{h}", c))
                    act.wait_ge(m_full[bank], use)
                    act.activation(bc[:, par, cut], mb[0:96, bank, :], ACT.Copy).then_inc(bc_hi, 1)
                elif name == "prep_mid":
                    for q in range(2):
                        bank, use = banks(kind, b, (f"prep_bc{q}", c))
                        act.wait_ge(m_free[bank], use)
                    act.activation(bc[32:64, par, :], rest[32:64, :], ACT.Copy)
                    act.activation(bc[64:96, par, :], rest[64:96, :], ACT.Copy).then_inc(bc_mid, 1)
                elif name in ("prep_dt0", "prep_dt1"):
                    act.wait_ge(x_silu, m + 1)
                    at_least(act, decayed, 16 * (m - 1))
                    at_least(act, u_done, m - 1)
                    bank, use = banks(kind, b, (name, c))
                    act.wait_ge(m_full[bank], use)
                    act.activation(e_x[:, cut], mb[:, bank, :], ACT.Abs, bias=col[:, C_DTB:C_DTB + 1]).then_inc(dt_abs, 1)
                    act.activation(dt[:, par, cut], mb[:, bank, :], ACT.Identity,
                                   bias=col[:, C_DTB:C_DTB + 1]).then_inc(m_free[bank], 1)
                elif name == "prep_dt_exp":
                    act.wait_ge(dt_abs, 2 * (m + 1))
                    act.activation(e_x[:], e_x[:], ACT.Exp, scale=-1.0).then_inc(dt_exp, 1)
                elif name == "prep_dt_one":
                    act.wait_ge(dt_exp, m + 1)
                    act.wait_ge(z_silu, m + 1)
                    act.activation(e_z[:], e_x[:], ACT.Identity, bias=1.0).then_inc(dt_one, 1)
                elif name == "prep_dt_ln":
                    if kind != "pro" and not (kind == FIRST and c == 0):
                        for q in range(2):
                            bank, use = banks(kind, b, (f"post_out{q}", c))
                            act.wait_ge(m_full[bank], use)
                    act.activation(yy[:], e_x[:], ACT.Ln, bias=1.0).then_inc(dt_ln, 1)
                elif name.startswith("a_rstd"):
                    g = int(name[-1])
                    act.wait_ge(v_mom[g], 3 * (t + 1))
                    rsqrt(gsm[:, 2, :], gsm[:, 1, :], gsm[:, 0, :], GN_EPS, a_rln[g], t + 1, a_rstd[g])
                elif name.startswith("a_affine"):
                    g, j = int(name[-2]), int(name[-1])
                    act.wait_ge(v_newton[g], 5 * (t + 1))
                    if g == 0:
                        act.wait_ge(s_x, 16 * (t + 1))
                        at_least(act, xn_done, NJ * t)
                        at_least(act, s_x2ld, 16 * b)
                    else:
                        act.wait_ge(x2_done, NJ * (t + 1))
                        at_least(act, s_xs[3], 32 * t)
                    act.activation((xn if g else cd)[:, j, :], xt[:, j, :], ACT.Square, scale=gsm[:, 4, j:j + 1],
                                   bias=gsm[:, 5, j:j + 1])
                    act.activation(gt[:, j, :], xt[:, j, :], ACT.Identity, scale=gsm[:, 4, j:j + 1],
                                   bias=gsm[:, 5, j:j + 1]).then_inc(a_sqd[g], 1)
                elif name == "a_rn":
                    bank, use = banks(kind, b, ("a_norm0", 0))
                    act.wait_ge(m_full[bank], use)
                    at_least(act, hot_done, 4 * t)
                    rsqrt(rn[:], rn_l[:], mb[:, bank, 0:NT], 0.0, rn_ln, t + 1, rn_done)
                    act.sem_inc(m_free[bank], 1)
                elif name.startswith("a_oht"):
                    q = int(name[-1])
                    bank, use = banks(kind, b, (f"a_turn{q}", 0))
                    act.wait_ge(m_full[bank], use)
                    src = mb[:, bank, :].bitcast(BF16).rearrange("p (k t) -> p k t", k=2)
                    act.activation(hot_t[:, :, q * HALF:(q + 1) * HALF], src, ACT.Copy).then_inc(hot_copied, 1)
                    act.wait_ge(hot_copied, 2 * t + q + 1)
                    act.sem_inc(m_free[bank], 1)
                elif name.startswith("c_sq"):
                    for q in range(2):
                        bank, use = banks(kind, b, (f"post_out{q}", 0))
                        act.wait_ge(m_free[bank], use)
                    act.wait_ge(s_x2ld, 16 * b)
                    act.activation(cd[:, h, :], ym[:, h, :], ACT.Square).then_inc(c_sqd, 1)
                elif name.startswith("a_xn"):
                    act.wait_ge(al_n, 2 * t + 2)
                    act.activation(xn[:, h, :], gt[:, h, :], ACT.Identity, scale=col[:, C_G + h:C_G + h + 1],
                                   bias=col[:, C_B + h:C_B + h + 1]).then_inc(xn_done, 1)
                elif name[2:5] == "msq":
                    own, s_sq, tt = ("a", al_sq, t) if name[0] == "a" else ("c", cl_sq, b - 1)
                    bank, use = banks(kind, b, (f"{own}_mean{h}", 0))
                    act.wait_ge(m_full[bank], use)
                    act.activation(sq[:], mb[:, bank, :], ACT.Square).then_inc(s_sq, 1)
                else:
                    own, s_ln, s_rs, tt = (("a", al_ln, al_rs, t) if name[0] == "a"
                                           else ("c", cl_ln, cl_rs, b - 1))
                    bank, use = banks(kind, b, (f"{own}_square{h}", 0))
                    act.wait_ge(m_free[bank], use)
                    rsqrt(rs[:, h, :], rs[:, h, :], rs[:, h, :], LN_EPS, s_ln, 2 * tt + h + 1, s_rs)

            def scan_operands(b, c, s):
                n16 = 64 * b + 16 * c
                k = BUF_OF_STATE[s]
                if s == 0:
                    act.wait_ge(dt_done, 4 * b + c + 1)
                at_least(act, scanned, n16 + last_use(BUF_OF_STATE, s) + 1)
                act.activation(decay[:, k, :], dt[:, c % 2, :], ACT.Exp, scale=a_neg[:, s:s + 1]).then_inc(decayed, 1)
                at_least(act, hc_done, n16 + s - 1)
                for h in range(2):
                    act.wait_ge(c_full, 2 * n16 + 2 * s + h + 1)
                    act.activation(c_sb[:, s % 2, h * HALF:(h + 1) * HALF], cb[:, h, :], ACT.Copy).then_inc(c_copied, 1)
                    yield h

            def turn(kind, b):
                for c in range(NC):
                    for s in range(NS):
                        for h in scan_operands(b, c, s):
                            for name in plan(ACT_SEQ, ACT_BATCH, kind, c, 2 * s + h):
                                do(name, kind, b, c)

            act.preload_act_table_set("natural_log_exp_and_others")
            act.wait_ge(s_w, 16 * 15)
            act.activation(a_neg[:], col[:, C_ALOG:C_ALOG + NS], ACT.Exp)
            for k in range(2):
                last = act.activation(word_n[:, k, :], word_f[:, k, :], ACT.Square, accum_out=wn[:, 0, k:k + 1])
            last.then_inc(su_act, 1)
            act.wait_ge(su_act, 1)
            act.activation(wn[:, 1, :], wn[:, 0, :], ACT.Ln).then_inc(su_act, 1)
            act.wait_ge(su_act, 2)
            act.activation(wn[:, 2, :], wn[:, 1, :], ACT.Exp, scale=-0.5).then_inc(su_act, 1)
            act.wait_ge(su_done, 1)
            for name in ("a_rstd0", "a_affine00", "a_affine01", "a_rn", "a_oht0", "a_oht1",
                         "a_rstd1", "a_affine10", "a_affine11", "a_msq0", "a_rs0", "a_msq1", "a_rs1", "a_xn0", "a_xn1"):
                do(name, "pro", -1, 0)
            for name in ("prep_xc0", "prep_xc1", "prep_z0", "prep_z1", "prep_sig_x", "prep_sig_z", "prep_hi0",
                         "prep_hi1", "prep_mid", "prep_dt0", "prep_dt1", "prep_dt_exp", "prep_dt_one", "prep_dt_ln"):
                do(name, "pro", -1, NC - 1)
            turn(FIRST, 0)
            with act.Fori(1, NB - 1) as b:
                turn(LOOP, b)
            turn(LAST, NB - 1)
            for name in ("c_sq0", "c_sq1", "c_msq0", "c_rs0", "c_msq1", "c_rs1"):
                do(name, "tail", NB, 0)

        @block.vector
        def _(dve):
            def chain(sem_, before):
                n = [0]

                def link(ins):
                    n[0] += 1
                    ins.then_inc(sem_, 1)
                    dve.wait_ge(sem_, before + n[0])
                    hold_here(dve)
                return link

            def do(name, kind, b, c):
                m = 4 * b + c + 1
                par = (c + 1) % 2
                t = b + 1
                if name.startswith("post_y"):
                    h = int(name[-1])
                    cut = slice(h * HALF, (h + 1) * HALF)
                    dve.wait_ge(summed, 32 * (m - 1) + h - 1)
                    at_least(dve, dt_done, m - 1)
                    dve.scalar_tensor_tensor(out=yy[:, cut], in0=xc[:, par, cut], scalar=col[:, C_D:C_D + 1],
                                             in1=yp[:, h, :], op0=ALU.mult, op1=ALU.add).then_inc(y_taken, 1)
                elif name.startswith("post_gate"):
                    h = int(name[-1])
                    cut = slice(h * HALF, (h + 1) * HALF)
                    dve.wait_ge(z_silu, m - 1)
                    dve.wait_ge(y_taken, 2 * (m - 2) + h + 1)
                    dve.tensor_tensor(yy[:, cut], yy[:, cut], zz[:, par, cut], ALU.mult).then_inc(y_gated, 1)
                elif name.startswith("post_skip"):
                    h = int(name[-1])
                    q = (c - 1) % NC
                    lo = DM * (q % 2)
                    bank, use = banks(kind, b, (f"post_out{h}", c))
                    dve.wait_ge(m_full[bank], use)
                    if c == 1:
                        if kind != FIRST:
                            mean_bank, mean_use = banks(kind, b, ("c_mean1", 0))
                            dve.wait_ge(m_free[mean_bank], mean_use)
                    start = PAD + q % 2 + h * HALF
                    dve.scalar_tensor_tensor(
                        out=ym[lo:lo + DM, q // 2, h * HALF:(h + 1) * HALF],
                        in0=xs[lo:lo + DM, q, start:start + HALF],
                        scalar=col[lo:lo + DM, C_SKIP:C_SKIP + 1], in1=mb[lo:lo + DM, bank, :],
                        op0=ALU.mult, op1=ALU.add).then_inc(m_free[bank], 1)
                elif name == "prep_clamp_x":
                    dve.wait_ge(x_pre, 2 * (m + 1))
                    dve.tensor_scalar(e_x[:], e_x[:], E_MAX, None, ALU.min).then_inc(x_clamped, 1)
                elif name == "prep_clamp_z":
                    dve.wait_ge(z_pre, 2 * (m + 1))
                    dve.tensor_scalar(e_z[:], e_z[:], E_MAX, None, ALU.min).then_inc(z_clamped, 1)
                elif name.startswith("prep_rest"):
                    h = int(name[-1])
                    at_least(dve, bc_lo, m)
                    bank, use = banks(kind, b, (f"prep_bc{h}", c))
                    cut = slice(h * HALF, (h + 1) * HALF)
                    dve.wait_ge(bc_hi, 2 * m + h + 1)
                    dve.tensor_tensor(rest[:, cut], mb[0:96, bank, :], bc[:, par, cut],
                                      ALU.subtract).then_inc(m_free[bank], 1)
                elif name == "prep_dt_err":
                    dve.wait_ge(dt_one, m + 1)
                    dve.scalar_tensor_tensor(out=e_z[:], in0=e_z[:], scalar=1.0, in1=e_x[:],
                                             op0=ALU.subtract, op1=ALU.subtract).then_inc(v_dt, 1)
                elif name == "prep_dt_log":
                    dve.wait_ge(dt_ln, m + 1)
                    dve.wait_ge(v_dt, 2 * m + 1)
                    dve.tensor_tensor(yy[:], yy[:], e_z[:], ALU.subtract).then_inc(v_dt, 1)
                elif name == "prep_dt_sum":
                    dve.wait_ge(v_dt, 2 * m + 2)
                    dve.scalar_tensor_tensor(out=dt[:, par, :], in0=dt[:, par, :], scalar=0.0, in1=yy[:],
                                             op0=ALU.max, op1=ALU.add).then_inc(dt_done, 1)
                elif name.startswith("a_stat"):
                    g, j = int(name[-2]), int(name[-1])
                    if g == 0:
                        dve.wait_ge(s_x, 16 * (t + 1))
                    else:
                        dve.wait_ge(x2_done, NJ * t + j + 1)
                    link = chain(v_stat[g], 6 * t + 3 * j)
                    for h in range(2):
                        last = dve.bn_stats(stats[:, j, h, :], xt[:, j, h * HALF:(h + 1) * HALF])
                    link(last)
                    link(dve.bn_aggr(mv[:, j, :], stats[:, j, :, :]))
                    dve.tensor_copy(gs[:, 0, j:j + 1], mv[:, j, 0:1])
                    link(dve.scalar_tensor_tensor(out=gs[:, 1, j:j + 1], in0=mv[:, j, 0:1], scalar=mv[:, j, 0:1],
                                                  in1=mv[:, j, 1:2], op0=ALU.mult, op1=ALU.add))
                elif name.startswith("a_mom"):
                    g = int(name[-1])
                    bank, use = banks(kind, b, (f"a_group{g}", 0))
                    link = chain(v_mom[g], 3 * t)
                    dve.wait_ge(m_full[bank], use)
                    link(dve.tensor_copy(gm[:].rearrange("p a j -> p (a j)"), mb[:, bank, 0:2 * NJ]))
                    dve.sem_inc(m_free[bank], 1)
                    link(dve.tensor_tensor(gsm[:, 3, :], gm[:, 0, :], gm[:, 0, :], ALU.mult))
                    link(dve.tensor_tensor(gsm[:, 0, :], gm[:, 1, :], gsm[:, 3, :], ALU.subtract))
                elif name.startswith("a_newton"):
                    g = int(name[-1])
                    dve.wait_ge(a_rstd[g], t + 1)
                    link = chain(v_newton[g], 5 * t)
                    link(dve.tensor_tensor(gsm[:, 3, :], gsm[:, 2, :], gsm[:, 2, :], ALU.mult))
                    link(dve.scalar_tensor_tensor(out=gsm[:, 6, :], in0=gsm[:, 0, :], scalar=GN_EPS,
                                                  in1=gsm[:, 3, :], op0=ALU.add, op1=ALU.mult))
                    link(dve.tensor_scalar(gsm[:, 7, :], gsm[:, 6, :], -0.5, 1.5, ALU.mult, ALU.add))
                    link(dve.tensor_tensor(gsm[:, 4, :], gsm[:, 2, :], gsm[:, 7, :], ALU.mult))
                    link(dve.scalar_tensor_tensor(out=gsm[:, 5, :], in0=gm[:, 0, :], scalar=-1.0,
                                                  in1=gsm[:, 4, :], op0=ALU.mult, op1=ALU.mult))
                elif name.startswith("a_pick"):
                    i = int(name[-1])
                    bank, use = banks(kind, b, (f"a_sim{i}0", 0))
                    dve.wait_ge(rn_done, t + 1)
                    dve.wait_ge(m_full[bank], use)
                    at_least(dve, hot_copied, 2 * t + i // 2 - 1)
                    link = chain(v_pick, 4 * (4 * t + i))
                    for k in range(2):
                        last = dve.tensor_scalar(sim[:, k, :], mb[:, bank, k * WORDS:(k + 1) * WORDS],
                                                 rn[:, 2 * i + k:2 * i + k + 1], 1.0, ALU.mult, ALU.subtract)
                    link(last)
                    dve.sem_inc(m_free[bank], 1)
                    for k in range(2):
                        last = dve.max(best[:, k, :], sim[:, k, :])
                    link(last)
                elif name.startswith("a_hot"):
                    i = int(name[-1])
                    link = chain(v_pick, 4 * (4 * t + i) + 2)
                    for k in range(2):
                        dve.max_index(where[:, k, :], best[:, k, :], sim[:, k, :])
                    link(dve.tensor_scalar(close[:], best[:, :, 0], -1.25, None, ALU.is_gt))
                    link(dve.tensor_copy(wheref[:], where[:, :, 0]))
                    for k in range(2):
                        last = dve.tensor_scalar(hot[:, 2 * i + k, :], iot[:], wheref[:, k:k + 1], close[:, k:k + 1],
                                                 ALU.is_equal, ALU.mult)
                    last.then_inc(hot_done, 1)
                elif name.startswith("a_keep"):
                    h = int(name[-1])
                    dve.wait_ge(xg_done, NJ * (t + 1))
                    bank, use = banks(kind, b, (name, 0))
                    dve.wait_ge(m_full[bank], use)
                    for j in range(NJ):
                        v = gt[:, j, h * HALF:(h + 1) * HALF]
                        last = dve.tensor_tensor(v, v, mb[:, bank, :], ALU.mult)
                    last.then_inc(m_free[bank], 1)
                elif name.startswith("a_mix"):
                    h, j = int(name[-2]), int(name[-1])
                    v = gt[:, j, h * HALF:(h + 1) * HALF]
                    bank, use = banks(kind, b, (name.replace("mix", "word"), 0))
                    dve.wait_ge(m_full[bank], use)
                    kept_bank, kept_use = banks(kind, b, (f"a_keep{h}", 0))
                    dve.wait_ge(m_free[kept_bank], kept_use)
                    dve.tensor_tensor(v, mb[:, bank, :], v, ALU.subtract).then_inc(m_free[bank], 1)
                elif name.startswith("c_out"):
                    h, mm = int(name[-2]), int(name[-1])
                    cut = slice(h * HALF, (h + 1) * HALF)
                    dve.wait_ge(s_x2ld, 16 * b)
                    bank, use = banks(kind, b, (name.replace("out", "proj"), 0))
                    dve.wait_ge(m_full[bank], use)
                    dve.scalar_tensor_tensor(out=res[:, mm, cut], in0=mb[:, bank, :], scalar=pb2[:, mm:mm + 1],
                                             in1=res[:, mm, cut], op0=ALU.add, op1=ALU.add).then_inc(m_free[bank], 1)
                elif name[2:5] == "var":
                    h = int(name[-1])
                    own, s_sq, s_other, others, tt = (
                        ("a", al_sq, cl_n, 2 * b, t) if name[0] == "a"
                        else ("c", cl_sq, al_n, 2 * (NB if kind == "tail" else t), b - 1))
                    bank1, use1 = banks(kind, b, (f"{own}_square{h}", 0))
                    dve.wait_ge(m_full[bank1], use1)
                    dve.wait_ge(s_sq, 2 * tt + h + 1)
                    at_least(dve, s_other, others)
                    dve.tensor_tensor(rs[:, h, :], mb[:, bank1, :], sq[:], ALU.subtract).then_inc(m_free[bank1], 1)
                elif name[2:5] == "ctr":
                    h = int(name[-1])
                    src, dst, own, s_sq, tt = ((gt, gt, "a", al_sq, t) if name[0] == "a"
                                               else (ym, cd, "c", cl_sq, b - 1))
                    bank0, use0 = banks(kind, b, (f"{own}_mean{h}", 0))
                    dve.wait_ge(m_full[bank0], use0)
                    dve.wait_ge(s_sq, 2 * tt + h + 1)
                    for j in range(NJ):
                        last = dve.tensor_tensor(dst[:, j, h * HALF:(h + 1) * HALF], src[:, j, h * HALF:(h + 1) * HALF],
                                                 mb[:, bank0, :], ALU.subtract)
                    last.then_inc(m_free[bank0], 1)

            def multiply(b, c, j):
                h = j % 2
                n32 = 128 * b + 32 * c
                if j == 0:
                    dve.wait_ge(u_done, 4 * b + c + 1)
                at_least(dve, scanned, 64 * b + 16 * c + j // 2 - 1)
                dve.wait_ge(b_full, n32 + j + 1)
                cut = slice(h * HALF, (h + 1) * HALF)
                dve.tensor_tensor(bx[:, (j // 2) % 2, cut], bb[:, h, :], u[:, c % 2, cut],
                                  ALU.mult).then_inc(bx_done, 1)

            def scan(b, c, s):
                n16 = 64 * b + 16 * c
                k = BUF_OF_STATE[s]
                dve.wait_ge(bx_done, 2 * (n16 + s + 1))
                dve.wait_ge(decayed, n16 + s + 1)
                at_least(dve, hc_done, n16 + last_use(BUF_OF_STATE, s) + 1)
                dve.tensor_tensor_scan(state[:, k, :], decay[:, k, :], bx[:, s % 2, :], 0.0,
                                       ALU.mult, ALU.add).then_inc(scanned, 1)

            def turn(kind, b):
                for c in range(NC):
                    for j in range(SEQ_STEPS):
                        multiply(b, c, j)
                        if j % 2 == 0 and j:
                            scan(b, c, j // 2 - 1)
                        for name in plan(DVE_SEQ, DVE_BATCH, kind, c, j):
                            do(name, kind, b, c)
                    scan(b, c, NS - 1)

            link = chain(su_dve, 0)
            dve.memset(oneb[:], 1.0)
            dve.memset(onef[:], 1.0)
            dve.memset(mean_w[:], 1.0 / CH)
            dve.wait_ge(s_w, 16 * 15)
            for k in range(2):
                dve.tensor_tensor(wtap[:, k, :], w_in_f, taps_f[:, k, :], ALU.mult)
            dve.tensor_scalar(ncb[:], col[:, C_CONVB:C_CONVB + 1], -1.0, None, ALU.mult)
            link(dve.tensor_copy(word_hml[:, 0, :, :], word_f))
            dve.sem_inc(su_pe_ready, 1)
            link(dve.tensor_tensor(word_r, word_f, word_hml[:, 0, :, :], ALU.subtract))
            link(dve.tensor_copy(word_hml[:, 1, :, :], word_r))
            link(dve.tensor_tensor(word_hml[:, 2, :, :], word_r, word_hml[:, 1, :, :], ALU.subtract))
            dve.wait_ge(su_act, 3)
            link(dve.tensor_tensor(wn[:, 3, :], wn[:, 2, :], wn[:, 2, :], ALU.mult))
            link(dve.tensor_tensor(wn[:, 4, :], wn[:, 3, :], wn[:, 0, :], ALU.mult))
            link(dve.tensor_scalar(wn[:, 5, :], wn[:, 4, :], -0.5, 1.5, ALU.mult, ALU.add))
            link(dve.tensor_tensor(wn[:, 6, :], wn[:, 2, :], wn[:, 5, :], ALU.mult))
            link(dve.tensor_scalar(word_q[:, 0, :], word_f[:, 0, :], wn[:, 6, 0:1], None, ALU.mult))
            link(dve.tensor_scalar(word_q[:, 1, :], word_f[:, 1, :], wn[:, 6, 1:2], None, ALU.mult))
            dve.sem_inc(su_words, 1)
            dve.wait_ge(m_full[0], 1)
            link(dve.tensor_copy(wdt[:], mb[:, 0, 0:P]))
            dve.sem_inc(m_free[0], 1)
            dve.wait_ge(m_full[1], 1)
            link(dve.tensor_tensor(pb2[:], mb[:, 1, 0:NJ], col[:, C_PB:C_PB + NJ], ALU.add))
            dve.sem_inc(m_free[1], 1)
            for j in range(NJ):
                link(dve.tensor_scalar(wp[:, j, :], wp[:, j, :], col[:, C_G + j:C_G + j + 1], None, ALU.mult))
            link(dve.tensor_scalar(a_neg[:], a_neg[:], -1.0, None, ALU.mult))
            for i in range(4):
                k, j = divmod(i, 2)
                bank, use = banks("pro", -1, ("word", i))
                dve.wait_ge(m_full[bank], use)
                link(dve.tensor_copy(wordn_t[:, j, k * P:(k + 1) * P], mb[:, bank, 0:P]))
                dve.sem_inc(m_free[bank], 1)
            dve.sem_inc(su_done, 1)

            for name in (["a_stat00", "a_stat01", "a_mom0", "a_newton0"] + [f"a_{w}{i}" for i in range(4) for w in ("pick", "hot")]
                         + ["a_keep0", "a_mix00", "a_mix01", "a_keep1", "a_mix10", "a_mix11", "a_stat10", "a_stat11", "a_mom1", "a_newton1",
                            "a_var0", "a_ctr0", "a_var1", "a_ctr1"]):
                do(name, "pro", -1, 0)
            for name in ("prep_clamp_x", "prep_clamp_z", "prep_rest0", "prep_rest1", "prep_dt_err", "prep_dt_log", "prep_dt_sum"):
                do(name, "pro", -1, NC - 1)
            turn(FIRST, 0)
            with dve.Fori(1, NB - 1) as b:
                turn(LOOP, b)
            turn(LAST, NB - 1)
            for name in ("post_y0", "post_y1", "post_gate0", "post_gate1", "post_skip0", "post_skip1", "c_var0", "c_ctr0", "c_var1", "c_ctr1", "c_out00", "c_out01", "c_out10", "c_out11"):
                do(name, "tail", NB, 0)

        @block.tensor
        def _(pe):
            def enter(kind, b, key):
                bank, use = banks(kind, b, key)
                at_least(pe, m_free[bank], use - 1)
                return bank

            def do(name, kind, b, c):
                m = 4 * b + c + 1
                cm = (c + 1) % NC
                bm = b + 1 if c == NC - 1 else b
                par = (c + 1) % 2
                t = b + 1
                h = int(name[-1]) if name[-1] in "01" else 0
                cut = slice(h * HALF, (h + 1) * HALF)
                if name.startswith("prep_xc"):
                    pe.wait_ge(s_xs[cm], 32 * (bm + 1))
                    bank = enter(kind, b, (name, c))
                    for k in range(2):
                        first = PAD - 2 * k + h * HALF
                        last = pe.matmul(mb[:, bank, :], wtap[:, k, :], xs[:, cm, first:first + HALF],
                                         start=(k == 0), stop=(k == 1))
                    last.then_inc(m_full[bank], 1)
                elif name.startswith("prep_z"):
                    bank = enter(kind, b, (name, c))
                    pe.matmul(mb[:, bank, :], wz[:], xs[0:DM, cm, PAD + h * HALF:PAD + (h + 1) * HALF],
                              start=True, stop=True).then_inc(m_full[bank], 1)
                elif name.startswith("prep_bc"):
                    pe.wait_ge(x_silu, m + 1)
                    bank = enter(kind, b, (name, c))
                    pe.matmul(mb[0:96, bank, :], wx[:], xc[:, par, cut], start=True, stop=True).then_inc(m_full[bank], 1)
                elif name.startswith("prep_dt"):
                    bank = enter(kind, b, (name, c))
                    pe.matmul(mb[:, bank, :], wdt[:], xc[:, par, cut], start=True, stop=True).then_inc(m_full[bank], 1)
                elif name.startswith("post_out"):
                    pe.wait_ge(y_gated, 2 * (m - 2) + h + 1)
                    lo = DM * ((c - 1) % 2)
                    bank = enter(kind, b, (name, c))
                    pe.matmul(mb[lo:lo + DM, bank, :], wo[:], yy[:, cut], start=True, stop=True).then_inc(m_full[bank], 1)
                elif name.startswith("a_group"):
                    pe.wait_ge(v_stat[h], 6 * (t + 1))
                    bank = enter(kind, b, (name, 0))
                    pe.matmul(mb[:, bank, 0:2 * NJ], grp[:], gs[:].rearrange("p a j -> p (a j)"),
                              start=True, stop=True).then_inc(m_full[bank], 1)
                elif name.startswith("a_norm"):
                    bank = banks(kind, b, ("a_norm0", 0))[0]
                    if h == 0:
                        pe.wait_ge(sq_added, t + 1)
                        enter(kind, b, (name, 0))
                    for i in range(h * NT // 2, (h + 1) * NT // 2):
                        last = pe.matmul(mb[:, bank, i:i + 1], cd[:, 0, i * P:(i + 1) * P], onef[:],
                                         start=True, stop=True)
                    if h == 1:
                        last.then_inc(m_full[bank], 1)
                elif name.startswith("a_sim"):
                    q, k = int(name[-2]), int(name[-1])
                    i = 2 * q + k
                    bank = banks(kind, b, (f"a_sim{q}0", 0))[0]
                    if k == 0:
                        enter(kind, b, (name, 0))
                    for j in range(NJ):
                        last = pe.matmul(mb[:, bank, k * WORDS:(k + 1) * WORDS], gt[:, j, i * P:(i + 1) * P],
                                         wordn_t[:, j, :], start=(j == 0), stop=(j == NJ - 1))
                    if k == 1:
                        last.then_inc(m_full[bank], 1)
                elif name.startswith("a_turn"):
                    q = int(name[-1])
                    pe.wait_ge(hot_done, 4 * t + 2 * q + 2)
                    bank = enter(kind, b, (name, 0))
                    dst = mb[:, bank, :].bitcast(BF16).rearrange("p (k t) -> p k t", k=2)
                    for i in range(4):
                        for k in range(2):
                            last = pe.transpose(dst[:, k, i * P:(i + 1) * P], hot[:, 4 * q + i, k * P:(k + 1) * P],
                                                idb[:])
                    last.then_inc(m_full[bank], 1)
                elif name.startswith("a_keep"):
                    h = int(name[-1])
                    pe.wait_ge(hot_copied, 2 * t + h + 1)
                    bank = enter(kind, b, (name, 0))
                    for k in range(2):
                        last = pe.matmul(mb[:, bank, :], oneb[:], hot_t[:, k, h * HALF:(h + 1) * HALF],
                                         start=(k == 0), stop=(k == 1))
                    last.then_inc(m_full[bank], 1)
                elif name.startswith("a_word"):
                    h, j = int(name[-2]), int(name[-1])
                    bank = enter(kind, b, (name, 0))
                    for i in range(6):
                        part, k = divmod(i, 2)
                        last = pe.matmul(mb[:, bank, :], word_hml[:, part, k, j * P:(j + 1) * P],
                                         hot_t[:, k, h * HALF:(h + 1) * HALF], start=(i == 0), stop=(i == 5))
                    last.then_inc(m_full[bank], 1)
                elif name.startswith("c_proj"):
                    h, mm = int(name[-2]), int(name[-1])
                    pe.wait_ge(cl_n, 2 * (b - 1) + h + 1)
                    bank = enter(kind, b, (name, 0))
                    for j in range(NJ):
                        last = pe.matmul(mb[:, bank, :], wp[:, j, mm * P:(mm + 1) * P],
                                         cd[:, j, h * HALF:(h + 1) * HALF], start=(j == 0), stop=(j == NJ - 1))
                    last.then_inc(m_full[bank], 1)
                else:
                    if name[0] == "a":
                        pe.wait_ge(a_sqd[1], NJ * (t + 1))
                        tile = gt if "mean" in name else xn
                    else:
                        pe.wait_ge(c_sqd, NJ * b)
                        tile = ym if "mean" in name else cd
                    bank = enter(kind, b, (name, 0))
                    for j in range(NJ):
                        last = pe.matmul(mb[:, bank, :], mean_w[:], tile[:, j, cut], start=(j == 0),
                                         stop=(j == NJ - 1))
                    last.then_inc(m_full[bank], 1)

            def broadcast(b, c, j):
                s, h = divmod(j, 2)
                n32 = 128 * b + 32 * c
                cut = slice(h * HALF, (h + 1) * HALF)
                if j == 0:
                    pe.wait_ge(bc_lo, 4 * b + c + 1)
                at_least(pe, bx_done, n32 + j - 1)
                pe.matmul(bb[:, h, :], sel[:, s, :], bc[:, c % 2, cut], start=True,
                          stop=True).then_inc(b_full, 1)
                at_least(pe, c_copied, n32 + j - 1)
                pe.matmul(cb[:, h, :], sel[:, NS + s, :], bc[:, c % 2, cut], start=True, stop=True).then_inc(c_full, 1)

            def sum_states(b, c, r):
                s, h = divmod(r, 2)
                n16 = 64 * b + 16 * c
                if s == 0:
                    at_least(pe, y_taken, 2 * (4 * b + c) + h - 1)
                pe.wait_ge(hc_done, n16 + s + 1)
                pe.matmul(yp[:, h, :], idf[:], hc[:, BUF_OF_STATE[s], h * HALF:(h + 1) * HALF],
                          start=(s == 0), stop=(s == NS - 1)).then_inc(summed, 1)

            def turn(kind, b):
                for c in range(NC):
                    for j in range(SEQ_STEPS):
                        broadcast(b, c, j)
                        for r in range(SEQ_STEPS):
                            if SUM_AT[r] == j:
                                sum_states(b, c, r)
                            elif SUM_AT[r] == j + SEQ_STEPS and not (kind == FIRST and c == 0):
                                sum_states(b if c else b - 1, (c - 1) % NC, r)
                        for name in plan(PE_SEQ, PE_BATCH, kind, c, j):
                            do(name, kind, b, c)

            pe.wait_ge(s_w, 16 * 15)
            pe.wait_ge(su_pe_ready, 1)
            pe.matmul(mb[:, 0, 0:P], wdt4[:, 1, :], wdt4[:, 0, :], start=True, stop=True).then_inc(m_full[0], 1)
            for mm in range(NJ):
                for j in range(NJ):
                    last = pe.matmul(mb[:, 1, mm:mm + 1], wp[:, j, mm * P:(mm + 1) * P], col[:, C_B + j:C_B + j + 1],
                                     start=(j == 0), stop=(j == NJ - 1))
            last.then_inc(m_full[1], 1)
            pe.wait_ge(su_words, 1)
            for i in range(4):
                k, j = divmod(i, 2)
                bank = enter("pro", -1, ("word", i))
                pe.transpose(mb[:, bank, 0:P], word_q[:, k, j * P:(j + 1) * P], idf[:]).then_inc(m_full[bank], 1)
            pe.wait_ge(su_done, 1)
            for name in A_ALL:
                do(name, "pro", -1, 0)
            for name in PREP_ALL:
                do(name, "pro", -1, NC - 1)
            turn(FIRST, 0)
            with pe.Fori(1, NB - 1) as b:
                turn(LOOP, b)
            turn(LAST, NB - 1)
            for r in range(SEQ_STEPS):
                if SUM_AT[r] >= SEQ_STEPS:
                    sum_states(NB - 1, NC - 1, r)
            for name in ["post_out0", "post_out1"] + C_STATS + C_PROJ:
                do(name, "tail", NB, 0)


def kernel(**inputs):
    import ml_dtypes
    import numpy as np
    import concourse.bacc as _bacc
    from concourse.bass_utils import run_bass_kernel_spmd as _run

    g = {k.replace("L1_conv_", ""): np.asarray(v) for k, v in inputs.items()}
    x_proj = g["x_proj_w"]
    cols = np.concatenate([
        g["conv_b"].reshape(P, 1), g["dt_proj_b"].reshape(P, 1), g["D_param"].reshape(P, 1), g["A_log"],
        g["norm_g"].reshape(NJ, P).T, g["norm_b"].reshape(NJ, P).T, g["proj_b"].reshape(NJ, P).T,
        np.broadcast_to(g["skip_scale"].reshape(1, 1), (P, 1))], axis=1)
    w_in_t = g["in_proj_w"][:P].T
    taps = g["conv_w"].T
    w_taps = np.empty((P, 2, P), taps.dtype)
    for k in range(2):
        w_taps[:DM, k] = taps[3 - 2 * k]
        w_taps[DM:, k] = taps[2 - 2 * k]
    select = np.zeros((96, 2 * NS, P), ml_dtypes.bfloat16)
    for r in range(96):
        select[r, r % 32] = 1
    arrays = {
        "x": g["x"], "words": g["L0_conv_negative_dict"], "cols": cols,
        "w_in": np.concatenate([w_in_t, w_in_t], axis=0), "w_z": g["in_proj_w"][P:].T, "w_taps": w_taps,
        "w_x": np.concatenate([x_proj[4:].T] * 3, axis=1), "w_dt": g["dt_proj_w"].T, "w_xdt": x_proj[:4],
        "w_out": g["out_proj_w"].T, "w_proj": g["proj_w"].T,
        "iota": np.broadcast_to(np.arange(WORDS, dtype=np.float32), (P, WORDS)),
        "ident_f": np.eye(P, dtype=np.float32), "ident_b": np.eye(P, dtype=ml_dtypes.bfloat16),
        "group_mean": np.kron(np.eye(P // 8, dtype=np.float32), np.full((8, 8), 0.125, np.float32)),
        "select": select,
    }
    nc = _bacc.Bacc("TRN2", target_bir_lowering=False, num_devices=1)
    named, args = {}, []
    for name, a in arrays.items():
        a = np.ascontiguousarray(a)
        named[f"in_{name}"] = a
        args.append(nc.dram_tensor(f"in_{name}", a.shape, mybir.dt.from_np(a.dtype), kind="ExternalInput").ap())
    out = nc.dram_tensor("out", (NB, CH, 32, 32), F32, kind="ExternalOutput").ap()
    build(nc, *args, out)
    r = _run(nc, [named], core_ids=[0])
    return r.results[0]["out"]
```
